# Optimizing a Trainium2 kernel written in Bass

```python
import numpy as np
import jax
import jax.numpy as jnp

def _softmax(x, axis=-1):
    return jax.nn.softmax(x, axis=axis)

def _gelu(x):
    return jax.nn.gelu(x, approximate=True)

def _silu(x):
    return jax.nn.silu(x)

def _sigmoid(x):
    return jax.nn.sigmoid(x)

def _layernorm(x, axis=-1, eps=1e-05):
    m = jnp.mean(x, axis=axis, keepdims=True)
    v = jnp.var(x, axis=axis, keepdims=True)
    return (x - m) / jnp.sqrt(v + eps)

def _scatter_add(tgt, idx, src, axis=0):
    return tgt.at[idx].add(src)

def _segment_sum(src, seg, n):
    return jax.ops.segment_sum(src, seg, n)
kernel_name = 'mk_adj_preln_d1_adj_r2_a637f5'

def setup_inputs(seed: int=0):
    np.random.seed(seed)
    _w = jnp.asarray

    def _rec_inputs():
        import jax
        import jax.numpy as jnp
        _gk = jax.random.key(seed)
        x = -0.0005207 + 1.001 * jax.random.normal(jax.random.fold_in(_gk, 1), (4096, 256), jnp.float32)
        _a = jax.random.bernoulli(jax.random.fold_in(_gk, 2), 0.00390625, (4096, 4096))
        _af = _a.astype(jnp.float32)
        adj = _af
        return (x, adj)
    x, adj = _rec_inputs()

    def _L0_gnn_setup():
        import jax, jax.numpy as jnp
        import numpy as np
        N = 2048
        INPUT_DIM = 256
        KEY_DIM = 64
        OUT_DIM = 256
        N_HEADS = 8
        IDENTITY_BIAS = 0.01
        MASK_VAL = 1e+16

        def _xavier(key, shape, gain=np.sqrt(2.0)):
            std = gain * np.sqrt(2.0 / (shape[-2] + shape[-1]))
            return jax.random.normal(key, shape, dtype=jnp.float32) * np.float32(std)
        key = jax.random.key(seed)
        kx, ka, kk, kq, kv, ko = jax.random.split(key, 6)
        node_matrix = jax.random.normal(kx, (N, INPUT_DIM), dtype=jnp.float32)
        adjacency_matrix = jax.random.bernoulli(ka, 0.01, (N, N)).astype(jnp.float32)
        Wks = _xavier(kk, (N_HEADS, INPUT_DIM, KEY_DIM))
        Wqs = _xavier(kq, (N_HEADS, INPUT_DIM, KEY_DIM))
        Wvs = _xavier(kv, (N_HEADS, INPUT_DIM, KEY_DIM))
        Wo = _xavier(ko, (N_HEADS, KEY_DIM, OUT_DIM))
        return {'node_matrix': node_matrix, 'adjacency_matrix': adjacency_matrix, 'Wks': Wks, 'Wqs': Wqs, 'Wvs': Wvs, 'Wo': Wo}
    _L0_gnn_all = _L0_gnn_setup()
    _L0_gnn_in = {k: v for k, v in _L0_gnn_all.items() if k in ('Wks', 'Wqs', 'Wvs', 'Wo')}
    del _L0_gnn_all
    return {'x': x, 'adj': adj, 'L0_gnn_Wks': _L0_gnn_in['Wks'], 'L0_gnn_Wqs': _L0_gnn_in['Wqs'], 'L0_gnn_Wvs': _L0_gnn_in['Wvs'], 'L0_gnn_Wo': _L0_gnn_in['Wo']}

def reference(x, adj, L0_gnn_Wks, L0_gnn_Wqs, L0_gnn_Wvs, L0_gnn_Wo):
    import jax
    import jax.numpy as jnp

    def _L0_gnn_ref(node_matrix, adjacency_matrix, Wks, Wqs, Wvs, Wo):
        import jax, jax.numpy as jnp
        import numpy as np
        N = 2048
        INPUT_DIM = 256
        KEY_DIM = 64
        OUT_DIM = 256
        N_HEADS = 8
        IDENTITY_BIAS = 0.01
        MASK_VAL = 1e+16

        def _xavier(key, shape, gain=np.sqrt(2.0)):
            std = gain * np.sqrt(2.0 / (shape[-2] + shape[-1]))
            return jax.random.normal(key, shape, dtype=jnp.float32) * np.float32(std)
        n = node_matrix.shape[0]
        kd = Wks.shape[-1]
        eye = jnp.eye(n, dtype=node_matrix.dtype)
        adj = jnp.maximum(adjacency_matrix, eye)
        q = jnp.einsum('nd,hdk->hnk', node_matrix, Wqs)
        k = jnp.einsum('nd,hdk->hnk', node_matrix, Wks)
        v = jnp.einsum('nd,hdk->hnk', node_matrix, Wvs)
        scores = jnp.einsum('hqk,hmk->hqm', q, k) * kd ** (-0.5)
        scores = scores + IDENTITY_BIAS * eye - MASK_VAL * (1.0 - adj)
        att = jax.nn.softmax(scores, axis=-1)
        return jnp.einsum('hqm,hmk,hko->qo', att, v, Wo)
    h = jnp.maximum(_layernorm(x, axis=-1), 0.0)
    x = x + _L0_gnn_ref(h, adj, L0_gnn_Wks, L0_gnn_Wqs, L0_gnn_Wvs, L0_gnn_Wo)
    return x

_drawn_inputs = setup_inputs


def setup_inputs(seed=0):
    import zlib

    import numpy as np

    out = dict(_drawn_inputs(seed))
    spreads = {}
    factors = {}
    for name, (base, spread) in spreads.items():
        noise = np.random.default_rng([zlib.crc32(name.encode()), seed]).standard_normal(out[name].shape)
        drawn = base * np.exp(spread * noise) if base else spread * noise
        out[name] = jnp.asarray(drawn.astype(out[name].dtype))
    for name, factor in factors.items():
        out[name] = (out[name] * factor).astype(out[name].dtype)
    return out
```

```python
from contextlib import ExitStack

import concourse.bass as bass
from concourse import mybir
from concourse.alu_op_type import AluOpType as ALU

ACT = mybir.ActivationFunctionType
AX_X = mybir.AxisListType.X
F32 = mybir.dt.float32
F32R = mybir.dt.float32r
BF16 = mybir.dt.bfloat16

N, D, HEADS, KD = 4096, 256, 8, 64
P = 128
DC = D // P
GROUP = 4
GROUPS = HEADS // GROUP
QT = 2
QW = QT * P
PAIRS = N // QW
STEPS = PAIRS * GROUP
MT = N // P
SLOT = 1024
SPT = N // SLOT
SLOTS = QT * SPT
TS = MT // 2
RING = 4
BANK = 512
CH = 512
EPS = 1e-5
SCALE = float(KD) ** -0.5
IDENTITY_BIAS = 0.01
MASK_VAL = 1e16
LOWEST = -3.0e38

PLAN = [1, 2, 3, 4, 5, 6, 7, None]
QUERY_AT = 3


START = 1


def count(i, h, per, extra):
    return i * (GROUP * per) + (h * per + extra)


def wait_apart(engine, sem, value, passed):
    engine.wait_ge(sem, value)
    engine.sem_inc(passed, 1)


def blk_norm(nc, sem, x, hT, xb, stats, mv, rstd, half, hb, psT, ident):
    NB = N // CH
    R = CH // P
    x_v = x.rearrange("(n r p) d -> n p r d", p=P, r=R)
    x_in = [sem(f"x_in{b}") for b in range(2)]
    h_out = [sem(f"h_out{b}") for b in range(2)]
    consts, stat1, aggr, var_ready, rstd_ready = (sem(s) for s in ("n_consts", "n_stat1", "n_aggr", "n_var", "n_rstd"))
    normed, x_transposed, h_ready, passed = sem("normed"), sem("x_transposed"), sem("h_ready"), sem("n_passed")

    with nc.Block() as block:
        @block.sync
        def _(sp):
            def load(n, b):
                sp.dma_start(xb[b], x_v[bass.ds(n, 1), :, :, :].rearrange("a p r d -> p (a r) d")).then_inc(x_in[b], 16)

            load(0, 0)
            load(1, 1)
            with sp.Fori(0, NB // 2 - 1) as i:
                for b in range(2):
                    sp.wait_ge(x_transposed, i * 2 + b + 1)
                    load(i * 2 + (b + 2), b)

        @block.gpsimd
        def _(pool):
            with pool.Fori(0, NB // 2) as i:
                for b in range(2):
                    pool.wait_ge(var_ready, i * 2 + (b + 1))
                    nc.gpsimd.tensor_tensor(rstd[:, b, :], mv[:, b, :, 1], half[:, :], ALU.pow).then_inc(rstd_ready, 1)

        @block.vector
        def _(dve):
            nc.vector.memset(half[:, :], -0.5).then_inc(consts, 1)
            dve.wait_ge(consts, 1)
            with dve.Fori(0, NB // 2) as i:
                for b in range(2):
                    dve.wait_ge(x_in[b], i * 16 + 16)
                    for r in range(R):
                        nc.vector.bn_stats(stats[:, b, r, :], xb[b][:, r, :]).then_inc(stat1, 1)
                    for r in range(R):
                        wait_apart(dve, stat1, i * (2 * R) + (b * R + r + 1), passed)
                        nc.vector.bn_aggr(mv[:, b, r, :], stats[:, b, r, :]).then_inc(aggr, 1)
                    dve.wait_ge(aggr, i * (2 * R) + (b * R + R))
                    nc.vector.tensor_scalar(mv[:, b, :, 1], mv[:, b, :, 1], EPS, None, ALU.add).then_inc(var_ready, 1)
                    dve.wait_ge(rstd_ready, i * 2 + (b + 1))
                    for r in range(R):
                        last = nc.vector.tensor_scalar(xb[b][:, r, :], xb[b][:, r, :], mv[:, b, r, 0:1],
                                                       rstd[:, b, r:r + 1], ALU.subtract, ALU.mult)
                    last.then_inc(normed, 1)

        @block.tensor
        def _(pe):
            with pe.Fori(0, NB // 2) as i:
                for b in range(2):
                    pe.wait_ge(normed, i * 2 + (b + 1))
                    pe.wait_ge(h_ready, i * 2 + (b + START))
                    for c in range(DC):
                        for r in range(R):
                            last = nc.tensor.transpose(psT[c][:, r * P:(r + 1) * P], xb[b][:, r, c * P:(c + 1) * P],
                                                       ident[:, :])
                    last.then_inc(x_transposed, 1)

        @block.scalar
        def _(act):
            def one(i, b):
                act.wait_ge(x_transposed, i * 2 + (b + 1))
                for c in range(DC):
                    last = nc.scalar.activation(hb[b][:, c, :], psT[c][:, :], ACT.Relu)
                last.then_inc(h_ready, 1)
                act.wait_ge(h_ready, i * 2 + (b + 1 + START))
                act.dma_start(hT[:, :, bass.ds((i * 2 + b) * CH, CH)], hb[b]).then_inc(h_out[b], 16)

            act.sem_inc(h_ready, START)
            one(0, 0)
            one(0, 1)
            with act.Fori(1, NB // 2) as i:
                for b in range(2):
                    act.wait_ge(h_out[b], i * 16)
                    one(i, b)
            for b in range(2):
                act.wait_ge(h_out[b], 16 * (NB // 2))


def blk_keys_values(nc, sem, g, hT, Wq, Wk, Wv, Wo, K2, V, hc, wk, wv, wq, wo, psK, psV):
    NC = N // CH
    heads = slice(g * GROUP, (g + 1) * GROUP)
    w_in = sem(f"w_in{g}")
    h_in = [sem(f"h_in{g}{b}") for b in range(2)]
    k_proj, v_proj, k_hi, k_lo, v_act, v_dve = (sem(f"{s}{g}") for s in ("k_proj", "v_proj", "k_hi", "k_lo", "v_act", "v_dve"))

    with nc.Block() as block:
        @block.sync
        def _(sp):
            def load(n, b):
                sp.dma_start(hc[b], hT[:, :, bass.ds(n * CH, CH)]).then_inc(h_in[b], 16)

            load(0, 0)
            load(1, 1)
            with sp.Fori(0, NC // 2 - 1) as i:
                for b in range(2):
                    sp.wait_ge(v_proj, i * 4 + (2 * b + 2))
                    load(i * 2 + (b + 2), b)

        @block.scalar
        def _(act):
            for w, dst in ((Wk, wk), (Wq, wq)):
                for c in range(DC):
                    for copy in range(2):
                        act.dma_start(dst[:, c, :, copy * KD:(copy + 1) * KD],
                                      w[heads, c * P:(c + 1) * P, :].rearrange("h p k -> p h k")).then_inc(w_in, 16)
            for c in range(DC):
                act.dma_start(wv[:, c, :].rearrange("p (h k) -> p h k", k=KD),
                              Wv[heads, c * P:(c + 1) * P, :].rearrange("h p k -> p h k")).then_inc(w_in, 16)
            for copy in range(2):
                act.dma_start(wo[copy * KD:(copy + 1) * KD, :, :], Wo[heads, :, :].rearrange("h k d -> k h d")).then_inc(w_in, 16)
            act.sem_inc(v_act, START)
            with act.Fori(0, NC // 2) as i:
                for b in range(2):
                    for h in range(GROUP):
                        act.wait_ge(k_proj, i * (2 * GROUP) + (b * GROUP + h + 1))
                        nc.scalar.activation(K2[:, h, bass.ds((i * 2 + b) * CH, CH)], psK[h], ACT.Copy).then_inc(k_hi, 1)
                    act.wait_ge(v_proj, i * 4 + (2 * b + 1))
                    nc.scalar.activation(V[:, bass.ds((i * 2 + b) * 4, 2), :], psV[0][:, :].rearrange("p (a n) -> p a n", a=2),
                                         ACT.Copy).then_inc(v_act, 1)

        @block.vector
        def _(dve):
            dve.sem_inc(k_lo, START)
            dve.sem_inc(v_dve, START)
            with dve.Fori(0, NC // 2) as i:
                for b in range(2):
                    for h in range(GROUP):
                        dve.wait_ge(k_hi, i * (2 * GROUP) + (b * GROUP + h + 1))
                        lo = K2[KD:2 * KD, h, bass.ds((i * 2 + b) * CH, CH)]
                        hi = K2.bitcast(F32)[KD:2 * KD, h, bass.ds((i * 2 + b) * CH, CH)]
                        nc.vector.tensor_tensor(lo, psK[h][KD:2 * KD, :], hi, ALU.subtract).then_inc(k_lo, 1)
                    dve.wait_ge(v_proj, i * 4 + (2 * b + 2))
                    nc.vector.tensor_copy(V[:, bass.ds((i * 2 + b) * 4 + 2, 2), :],
                                          psV[1][:, :].rearrange("p (a n) -> p a n", a=2)).then_inc(v_dve, 1)

        @block.tensor
        def _(pe):
            pe.wait_ge(w_in, 16 * (4 * DC + DC + 2))
            with pe.Fori(0, NC // 2) as i:
                for b in range(2):
                    pe.wait_ge(h_in[b], i * 16 + 16)
                    pe.wait_ge(k_lo, i * (2 * GROUP) + (b * GROUP + START))
                    for h in range(GROUP):
                        for c in range(DC):
                            last = nc.tensor.matmul(psK[h], wk[:, c, h, :], hc[b][:, c, :], start=(c == 0), stop=(c == DC - 1))
                        last.then_inc(k_proj, 1)
                    for u, read in ((0, v_act), (1, v_dve)):
                        pe.wait_ge(read, i * 2 + (b + START))
                        for a in range(2):
                            m = 2 * u + a
                            for c in range(DC):
                                last = nc.tensor.matmul(psV[u][:, a * 256:(a + 1) * 256], hc[b][:, c, m * P:(m + 1) * P],
                                                        wv[:, c, :], start=(c == 0), stop=(c == DC - 1))
                        last.then_inc(v_proj, 1)


def blk_attention(nc, sem, g, hT, adj, base, result, K2, V, wq, wo, S, B, notI, diag, QH, QL, hq, PT, O, acc, res,
                  mx, negm, sums, den, rden, psS, psT, psO, psP, ident):
    hq_in, base_in, stored = sem(f"hq_in{g}"), sem(f"base_in{g}"), sem(f"stored{g}")
    dve_passed, pool_passed = sem(f"dve_passed{g}"), sem(f"pool_passed{g}")
    adj_in = [sem(f"adj_in{g}{k}") for k in range(SPT)]
    (bias_conv, bias_ready, q_proj, q_hi, q_lo, scores_ready, slot_masked, max_reduced, row_ready, probs_ready,
     transposed, pt_act, pt_dve, pt_free, o_ready, projected, summed, den_ready, head_added) = (
        sem(f"{s}{g}") for s in (
            "bias_conv", "bias_ready", "q_proj", "q_hi", "q_lo", "scores_ready", "slot_masked", "max_reduced", "row_ready",
            "probs_ready", "transposed", "pt_act", "pt_dve", "pt_free", "o_ready", "projected", "summed", "den_ready",
            "head_added"))

    def steps(engine, body):
        with engine.Fori(0, PAIRS - 1) as i:
            for h in range(GROUP):
                body(i, h, True, True)
        for h in range(GROUP):
            body(PAIRS - 1, h, h + 1 < GROUP, h + 2 < GROUP)

    with nc.Block() as block:
        @block.sync
        def _(sp):
            def load_hq(i):
                sp.dma_start(hq[:, :, :], hT[:, :, bass.ds(i * QW, QW)]).then_inc(hq_in, 16)

            def load_base(i):
                sp.dma_start(acc[:, :, :], base[bass.ds(i * QW, QW), :].rearrange("(a p) d -> p a d", p=P)).then_inc(base_in, 16)

            def store(i):
                sp.wait_ge(head_added, count(i, 3, 1, 1 + START))
                sp.dma_start(result[bass.ds(i * QW, QW), :].rearrange("(a p) d -> p a d", p=P), res[:, :, :]).then_inc(stored, 16)

            sp.sem_inc(stored, 16 * START)
            load_hq(0)
            load_base(0)
            with sp.Fori(0, PAIRS - 1) as i:
                sp.wait_ge(q_proj, count(i, 4, 1, 0))
                load_hq(i + 1)
                store(i)
                load_base(i + 1)
            store(PAIRS - 1)
            sp.wait_ge(stored, 16 * (PAIRS + START))

        @block.gpsimd
        def _(pool):
            def fill(i, first):
                for q in range(QT):
                    for k in range(SPT):
                        if not first:
                            pool.wait_ge(slot_masked, count(i, 0, SLOTS, 0) - (SLOTS - (q * SPT + k + 1)))
                        rows = adj[bass.ds(i * QW + q * P, P), k * SLOT:(k + 1) * SLOT]
                        pool.dma_start(B[:, q, k * SLOT:(k + 1) * SLOT], rows).then_inc(adj_in[k], 16)
                    for k in range(SPT):
                        wait_apart(pool, adj_in[k], i * (16 * QT) + 16 * (q + 1), pool_passed)
                        part = B[:, q, k * SLOT:(k + 1) * SLOT]
                        last = nc.gpsimd.tensor_scalar(part, part, -1.0, MASK_VAL / SCALE, ALU.add, ALU.mult)
                    last.then_inc(bias_conv, 1)
                    pool.wait_ge(bias_conv, i * QT + q + 1)
                    own = B[:, q, bass.ds(i * QW + q * P, P)]
                    nc.gpsimd.tensor_tensor(own, own, notI[:, :], ALU.mult).then_inc(bias_ready, 1)

            fill(0, True)
            with pool.Fori(1, PAIRS) as i:
                fill(i, False)

        @block.tensor
        def _(pe):
            def query(i, h, wait_hq, first):
                if wait_hq:
                    pe.wait_ge(hq_in, i * 16 + 16)
                pe.wait_ge(q_lo, count(i, h, 1, 0))
                if not first:
                    pe.wait_ge(head_added, count(i, h, 1, START - 2))
                for c in range(DC):
                    last = nc.tensor.matmul(psP[:, 0:QW], wq[:, c, h, :], hq[:, c, :], start=(c == 0), stop=(c == DC - 1))
                last.then_inc(q_proj, 1)

            def scores(i, h, j, first=False):
                q, k = divmod(j, SPT)
                if j == 0:
                    pe.wait_ge(q_hi, count(i, h, 1, 1))
                    pe.wait_ge(q_lo, count(i, h, 1, 1))
                if not (first and j < 2):
                    pe.wait_ge(slot_masked, count(i, h, SLOTS, j - 1))
                for part, hi in ((QH, True), (QL, False)):
                    for b in range(SLOT // BANK):
                        col = k * SLOT + b * BANK
                        last = nc.tensor.matmul(psS[j % 2][:, b * BANK:(b + 1) * BANK], part[:, h % 2, q * P:(q + 1) * P],
                                                K2[:, h, col:col + BANK], start=hi, stop=not hi)
                last.then_inc(scores_ready, 1)

            def transposes(i, h, s):
                if s % 4 == 0:
                    pe.wait_ge(probs_ready, count(i, h, SLOTS, SPT + s // 4 + 1))
                pe.wait_ge(pt_dve if s % 2 else pt_act, count(i, h, TS // 2, s // 2 + START))
                for a in range(2):
                    for q in range(QT):
                        col = (2 * s + a) * P
                        last = nc.tensor.transpose(psT[s % 2][:, a * QW + q * P:a * QW + (q + 1) * P],
                                                   S[:, h % 2, q, col:col + P], ident[:, :])
                last.then_inc(transposed, 1)

            def values(i, h, s):
                pe.wait_ge(pt_dve if s % 2 else pt_act, count(i, h, TS // 2, s // 2 + 1 + START))
                if s == 0:
                    pe.wait_ge(o_ready, count(i, h, 1, START))
                for a in range(2):
                    last = nc.tensor.matmul(psO[a * KD:(a + 1) * KD, 0:QW], V[:, 2 * s + a, h * KD:(h + 1) * KD],
                                            PT[:, s % RING, a * QW:(a + 1) * QW], start=(s == 0), stop=(s == TS - 1))
                last.then_inc(pt_free, 1)

            def project(i, h, nxt2):
                pe.wait_ge(o_ready, count(i, h, 1, 1 + START))
                pe.wait_ge(head_added, count(i, h, 1, START))
                if nxt2:
                    pe.wait_ge(q_lo, count(i, h, 1, 3))
                for q in range(QT):
                    last = nc.tensor.matmul(psP[:, q * D:(q + 1) * D], O[:, q * P:(q + 1) * P], wo[:, h, :], start=True, stop=True)
                last.then_inc(projected, 1)

            def step(i, h, nxt, nxt2):
                i1, h1 = (i, h + 1) if h + 1 < GROUP else (i + 1, 0)
                i2, h2 = (i, h + 2) if h + 2 < GROUP else (i + 1, h + 2 - GROUP)
                for c, j in enumerate(PLAN):
                    if nxt and j is not None:
                        scores(i1, h1, j)
                    transposes(i, h, 2 * c)
                    transposes(i, h, 2 * c + 1)
                    if c:
                        values(i, h, 2 * c - 2)
                        values(i, h, 2 * c - 1)
                    if nxt2 and c == QUERY_AT:
                        query(i2, h2, h2 == 0, False)
                values(i, h, TS - 2)
                values(i, h, TS - 1)
                if nxt2:
                    scores(i2, h2, 0)
                project(i, h, nxt2)

            pe.sem_inc(pt_free, RING)
            pe.sem_inc(projected, START)
            query(0, 0, True, True)
            query(0, 1, False, True)
            for j in range(SLOTS):
                scores(0, 0, j, True)
            scores(0, 1, 0)
            steps(pe, step)

        @block.scalar
        def _(act):
            def query_hi(i, h):
                act.wait_ge(q_proj, count(i, h, 1, 1))
                nc.scalar.activation(QH[:, h % 2, :], psP[:, 0:QW], ACT.Copy).then_inc(q_hi, 1)

            def exps(i, h, q, k):
                if k == 0:
                    act.wait_ge(row_ready, count(i, h, QT, q + 1))
                part = S[:, h % 2, q, k * SLOT:(k + 1) * SLOT]
                nc.scalar.activation(part, part, ACT.Exp, bias=negm[:, h % 2, q:q + 1],
                                     accum_out=sums[:, h % 2, q, k:k + 1]).then_inc(probs_ready, 1)

            def step(i, h, nxt, nxt2):
                i1, h1 = (i, h + 1) if h + 1 < GROUP else (i + 1, 0)
                i2, h2 = (i, h + 2) if h + 2 < GROUP else (i + 1, h + 2 - GROUP)
                for c in range(TS // 2):
                    s = 2 * c
                    act.wait_ge(transposed, count(i, h, TS, s + 1))
                    act.wait_ge(pt_free, count(i, h, TS, s + 1))
                    nc.scalar.activation(PT[:, s % RING, :], psT[0][:, :], ACT.Copy).then_inc(pt_act, 1)
                    if c % 2 == 0 and c < 6:
                        exps(i, h, 1, c // 2 + 1)
                    if nxt and c >= SPT:
                        exps(i1, h1, 0, c - SPT)
                    if nxt2 and c == QUERY_AT:
                        act.wait_ge(scores_ready, count(i, h, SLOTS, SLOTS))
                        query_hi(i2, h2)
                if nxt:
                    exps(i1, h1, 1, 0)
                act.wait_ge(pt_free, count(i, h, TS, TS + RING))
                act.wait_ge(projected, count(i, h, 1, START))
                nc.scalar.activation(O[:, :], psO[:, 0:QW], ACT.Copy).then_inc(o_ready, 1)

            act.sem_inc(pt_act, START)
            act.sem_inc(o_ready, START)
            query_hi(0, 0)
            query_hi(0, 1)
            for k in range(SPT):
                exps(0, 0, 0, k)
            exps(0, 0, 1, 0)
            steps(act, step)

        @block.vector
        def _(dve):
            def query_lo(i, h):
                dve.wait_ge(q_hi, count(i, h, 1, 1))
                nc.vector.tensor_tensor(QL[:, h % 2, :], psP[:, 0:QW], QH.bitcast(F32)[:, h % 2, :],
                                        ALU.subtract).then_inc(q_lo, 1)

            def mask(i, h, j):
                q, k = divmod(j, SPT)
                if h == 0 and k == 0:
                    dve.wait_ge(bias_ready, i * QT + (q + 1))
                wait_apart(dve, scores_ready, count(i, h, SLOTS, j + 1), dve_passed)
                part = S[:, h % 2, q, k * SLOT:(k + 1) * SLOT]
                nc.vector.tensor_tensor_reduce(out=part, in0=psS[j % 2][:, :], in1=B[:, q, k * SLOT:(k + 1) * SLOT],
                                               scale=SCALE, scalar=LOWEST, op0=ALU.add, op1=ALU.max,
                                               accum_out=mx[:, h % 2, q, k:k + 1]).then_inc(slot_masked, 1)
                if k == SPT - 1:
                    dve.wait_ge(slot_masked, count(i, h, SLOTS, j + 1))
                    own = S[:, h % 2, q, bass.ds(i * QW + q * P, P)]
                    nc.vector.tensor_tensor(own, own, diag[:, :], ALU.add)
                    nc.vector.tensor_reduce(negm[:, h % 2, q:q + 1], mx[:, h % 2, q, :], AX_X, ALU.max,
                                            negate=True).then_inc(row_ready, 1)

            def denominators(i, h):
                dve.wait_ge(probs_ready, count(i, h, SLOTS, SLOTS))
                nc.vector.tensor_reduce(den[:, :], sums[:, h % 2, :, :], AX_X, ALU.add).then_inc(summed, 1)
                dve.wait_ge(summed, count(i, h, 1, 1))
                nc.vector.reciprocal(rden[:, :], den[:, :]).then_inc(den_ready, 1)

            def add_head(i, h):
                dve.wait_ge(projected, count(i, h, 1, 1 + START))
                dve.wait_ge(den_ready, count(i, h, 1, 1))
                if h == 0:
                    dve.wait_ge(base_in, i * 16 + 16)
                else:
                    dve.wait_ge(head_added, count(i, h, 1, START))
                if h == GROUP - 1:
                    dve.wait_ge(stored, i * 16 + 16 * START)
                dst = res if h == GROUP - 1 else acc
                for q in range(QT):
                    last = nc.vector.scalar_tensor_tensor(out=dst[:, q, :], in0=psP[:, q * D:(q + 1) * D],
                                                          scalar=rden[:, q:q + 1], in1=acc[:, q, :],
                                                          op0=ALU.mult, op1=ALU.add)
                last.then_inc(head_added, 1)

            def step(i, h, nxt, nxt2):
                i1, h1 = (i, h + 1) if h + 1 < GROUP else (i + 1, 0)
                i2, h2 = (i, h + 2) if h + 2 < GROUP else (i + 1, h + 2 - GROUP)
                for c, j in enumerate(PLAN):
                    if nxt and j is not None:
                        mask(i1, h1, j)
                    s = 2 * c + 1
                    dve.wait_ge(transposed, count(i, h, TS, s + 1))
                    dve.wait_ge(pt_free, count(i, h, TS, s + 1))
                    nc.vector.tensor_copy(PT[:, s % RING, :], psT[1][:, :]).then_inc(pt_dve, 1)
                    if nxt2 and c == QUERY_AT:
                        query_lo(i2, h2)
                denominators(i, h)
                if nxt2:
                    mask(i2, h2, 0)
                add_head(i, h)

            dve.sem_inc(pt_dve, START)
            dve.sem_inc(head_added, START)
            query_lo(0, 0)
            query_lo(0, 1)
            for j in range(SLOTS):
                mask(0, 0, j)
            mask(0, 1, 0)
            steps(dve, step)


def build(nc, x, adj, Wk, Wq, Wv, Wo, out):
    hT = nc.dram_tensor("hT_scratch", [P, DC, N], F32, kind="Internal").ap()
    partial = nc.dram_tensor("partial_scratch", [N, D], F32, kind="Internal").ap()
    with ExitStack() as ctx:
        def sb(name, shape, dt=F32):
            return ctx.enter_context(nc.sbuf_tensor(name, shape, dt))

        def sem(name):
            return ctx.enter_context(nc.semaphore(name))

        K2 = sb("K2", [P, GROUP, N], F32R)
        V = sb("V", [P, MT, GROUP * KD])
        S = sb("S", [P, 2, QT, N])
        B = sb("B", [P, QT, N], BF16)
        PT = sb("PT", [P, RING, 2 * QW])
        QH = sb("QH", [P, 2, QW], F32R)
        QL = sb("QL", [P, 2, QW], F32R)
        hq = sb("hq", [P, DC, QW])
        wq = sb("wq", [P, DC, GROUP, 2 * KD])
        wo = sb("wo", [P, GROUP, D])
        O = sb("O", [P, QW])
        acc = sb("acc", [P, QT, D])
        res = sb("res", [P, QT, D])
        ident = sb("ident", [P, P])
        notI = sb("notI", [P, P], BF16)
        diag = sb("diag", [P, P])
        mx = sb("mx", [P, 2, QT, SPT])
        negm = sb("negm", [P, 2, QT])
        sums = sb("sums", [P, 2, QT, SPT])
        den = sb("den", [P, QT])
        rden = sb("rden", [P, QT])
        stats = sb("stats", [P, 2, CH // P, 6])
        mv = sb("mv", [P, 2, CH // P, 2])
        rstd = sb("rstd", [P, 2, CH // P])
        half = sb("half", [P, CH // P])
        psS = [ctx.enter_context(nc.psum_tensor(f"psS{j}", [P, SLOT], F32)) for j in range(2)]
        psT = [ctx.enter_context(nc.psum_tensor(f"psT{j}", [P, BANK], F32)) for j in range(2)]
        psO = ctx.enter_context(nc.psum_tensor("psO", [P, BANK], F32))
        psP = ctx.enter_context(nc.psum_tensor("psP", [P, BANK], F32))

        xb = [S[:, 0, 0, b * 1024:(b + 1) * 1024].rearrange("p (r d) -> p r d", d=D) for b in range(2)]
        hb = [S[:, 0, 1, b * 1024:(b + 1) * 1024].rearrange("p (c n) -> p c n", c=DC) for b in range(2)]
        hc = [S[:, 1, 0, b * 1024:(b + 1) * 1024].rearrange("p (c n) -> p c n", c=DC) for b in range(2)]
        wk = S[:, 1, 1, 0:1024].rearrange("p (c h k) -> p c h k", c=DC, h=GROUP)
        wv = S[:, 1, 1, 1024:1536].rearrange("p (c n) -> p c n", c=DC)
        psK = [psS[h // 2][:, (h % 2) * BANK:(h % 2 + 1) * BANK] for h in range(GROUP)]

        ones_set, consts = sem("ones_set"), sem("consts")
        with nc.Block() as block:
            @block.gpsimd
            def _(pool):
                nc.gpsimd.memset(ident[:, :], 0.0).then_inc(ones_set, 1)
                nc.gpsimd.memset(notI[:, :], 1.0).then_inc(ones_set, 1)
                nc.gpsimd.memset(diag[:, :], 0.0).then_inc(ones_set, 1)
                pool.wait_ge(ones_set, 3)
                for m, fill in ((ident, 1.0), (notI, 0.0), (diag, IDENTITY_BIAS)):
                    nc.gpsimd.affine_select(out=m[:, :], in_=m[:, :], compare_op=ALU.not_equal, fill=fill, base=0,
                                            pattern=[[-1, P]], channel_multiplier=1).then_inc(consts, 1)
                pool.wait_ge(consts, 3)

        blk_norm(nc, sem, x, hT, xb, stats, mv, rstd, half, hb, psT, ident)
        for g in range(GROUPS):
            blk_keys_values(nc, sem, g, hT, Wq, Wk, Wv, Wo, K2, V, hc, wk, wv, wq, wo, psK, psT)
            blk_attention(nc, sem, g, hT, adj, x if g == 0 else partial, out if g == GROUPS - 1 else partial,
                          K2, V, wq, wo, S, B, notI, diag, QH, QL, hq, PT, O, acc, res,
                          mx, negm, sums, den, rden, psS, psT, psO, psP, ident)


def kernel(x, adj, L0_gnn_Wks, L0_gnn_Wqs, L0_gnn_Wvs, L0_gnn_Wo):
    import concourse.bacc as bacc
    import numpy as np
    from concourse.bass_utils import run_bass_kernel_spmd

    nc = bacc.Bacc("TRN2", target_bir_lowering=False, num_devices=1)
    arrays, args = {}, []
    for name, a in (("x", x), ("adj", adj), ("Wk", L0_gnn_Wks), ("Wq", L0_gnn_Wqs), ("Wv", L0_gnn_Wvs), ("Wo", L0_gnn_Wo)):
        a = np.ascontiguousarray(a)
        arrays[f"in_{name}"] = a
        args.append(nc.dram_tensor(f"in_{name}", a.shape, mybir.dt.from_np(a.dtype), kind="ExternalInput").ap())
    out = nc.dram_tensor("out", [N, D], F32, kind="ExternalOutput").ap()
    build(nc, *args, out)
    r = run_bass_kernel_spmd(nc, [arrays], core_ids=[0])
    return r.results[0]["out"]
```

```python
from contextlib import ExitStack

import concourse.bass as bass
from concourse import mybir
from concourse.alu_op_type import AluOpType as ALU

ACT = mybir.ActivationFunctionType
AX_X = mybir.AxisListType.X
F32 = mybir.dt.float32
F32R = mybir.dt.float32r
BF16 = mybir.dt.bfloat16

N, D, HEADS, KD = 4096, 256, 8, 64
P = 128
DC = D // P
GROUP = 4
GROUPS = HEADS // GROUP
QT = 2
QW = QT * P
PAIRS = N // QW
STEPS = PAIRS * GROUP
MT = N // P
SLOT = 1024
SPT = N // SLOT
SLOTS = QT * SPT
LATE = SLOT // P
LC = N - LATE * P
TS = (MT - LATE) // 2
QUAD = P // 32
MOVES = QUAD * (QUAD - 1)
RING = 4
BANK = 512
CH = 512
CR = CH // P
NC = N // CH
EPS = 1e-5
SCALE = float(KD) ** -0.5
IDENTITY_BIAS = 0.01
MASK_VAL = 1e16
LOWEST = -3.0e38

SUBSTEPS = TS // 2
EXP_ORDER = [SPT - 1] + list(range(SPT - 1))
PROJECT_AT = 1
QUERY_AT = 3


START = 1


def count(i, h, per, extra):
    return i * (GROUP * per) + (h * per + extra)


def wait_apart(engine, sem, value, passed):
    engine.wait_ge(sem, value)
    engine.sem_inc(passed, 1)


def group_programs(nc, sem, g, before, x, hT, adj, Wk, Wq, Wv, Wo, base, result, t):
    (K2, V, S, B, PT, QH, QL, hq, wq, wo, O, Oodd, RB, acc, res, ident, notI, diag, mx, negm, sums, den, rden,
     stats, mv, rstd, half, xb, hc, wk, wv, psS, psT, psO, psP, rden_scratch) = t
    norm = g == 0
    heads = slice(g * GROUP, (g + 1) * GROUP)
    x_v = x.rearrange("(n r p) d -> n p r d", p=P, r=CR)
    psK = [[psS[pair][:, b * BANK:(b + 1) * BANK] for b in range(2)] for pair in range(GROUP // 2)]
    psV = [psO, psP]

    x_in = [sem(f"x_in{g}{b}") for b in range(2)]
    h_in = [sem(f"h_in{g}{b}") for b in range(2)]
    h_out = [sem(f"h_out{g}{b}") for b in range(2)]
    (w_in, wqo_in, half_set, stat1, aggr, var_ready, rstd_ready, normed, x_transposed, h_ready, k_proj, v_proj, k_hi, k_lo,
     v_act, v_dve) = (sem(f"{s}{g}") for s in (
         "w_in", "wqo_in", "half_set", "stat1", "aggr", "var_ready", "rstd_ready", "normed", "x_transposed", "h_ready",
         "k_proj", "v_proj", "k_hi", "k_lo", "v_act", "v_dve"))

    hq_in, base_in, stored = sem(f"hq_in{g}"), sem(f"base_in{g}"), sem(f"stored{g}")
    dve_passed, pool_passed = sem(f"dve_passed{g}"), sem(f"pool_passed{g}")
    adj_in = [[sem(f"adj_in{g}{q}{k}") for k in range(SPT)] for q in range(QT)]
    (bias_conv, bias_ready, q_proj, q_hi, q_lo, scores_ready, slot_masked, row_ready, probs_ready,
     transposed, pt_act, pt_dve, pt_free, o_ready, projected, summed, den_ready, head_added,
     late_transposed, late_moved, late_copied, late_used, odd_copied, o_summed, rden_stored, rden_in) = (
        sem(f"{s}{g}") for s in (
            "bias_conv", "bias_ready", "q_proj", "q_hi", "q_lo", "scores_ready", "slot_masked", "row_ready",
            "probs_ready", "transposed", "pt_act", "pt_dve", "pt_free", "o_ready", "projected", "summed", "den_ready",
            "head_added", "late_transposed", "late_moved", "late_copied", "late_used", "odd_copied", "o_summed",
            "rden_stored", "rden_in"))

    def chunks(engine, body):
        with engine.Fori(0, NC // 2 - 1) as i:
            for b in range(2):
                body(i, b, True, True)
        body(NC // 2 - 1, 0, True, False)
        body(NC // 2 - 1, 1, False, False)

    def after(i, b):
        return (i, 1) if b == 0 else (i + 1, 0)

    def T1(h):
        return S[:, (h + 1) % 2, 1, SLOT:3 * SLOT].rearrange("p (q n) -> p q n", q=QT)

    def last_step(i, h):
        return (i, h - 1) if h else (i - 1, GROUP - 1)

    def late_blocks(h, qi, qj):
        return (T1(h)[qi * 32:(qi + 1) * 32, :, qj * 256:(qj + 1) * 256],
                S[qj * 32:(qj + 1) * 32, h % 2, :, LC + qi * 256:LC + (qi + 1) * 256])

    def steps(engine, body):
        for h in range(GROUP):
            body(0, h, True, True, h > 0)
        with engine.Fori(1, PAIRS - 1) as i:
            for h in range(GROUP):
                body(i, h, True, True, True)
        for h in range(GROUP):
            body(PAIRS - 1, h, h + 1 < GROUP, h + 2 < GROUP, True)

    if not norm:
        late_used_before, slot_masked_before, projected_before, o_summed_before, head_added_before = before

    def sync_program(sp):
        def load_hq(i):
            sp.dma_start(hq[:, :, :], hT[:, :, bass.ds(i * QW, QW)]).then_inc(hq_in, 16)

        def load_x(i, b):
            sp.dma_start(xb[b], x_v[bass.ds(i * 2 + b, 1), :, :, :].rearrange("a p r d -> p (a r) d")).then_inc(x_in[b], 16)

        def load_h(i, b):
            sp.dma_start(hc[b], hT[:, :, bass.ds((i * 2 + b) * CH, CH)]).then_inc(h_in[b], 16)

        load = load_x if norm else load_h
        if not norm:
            sp.wait_ge(late_used_before, STEPS - 1)
        load(0, 0)
        for w, dst in ((Wk, wk), (Wv, wv)):
            for c in range(DC):
                sp.dma_start(dst[:, c, :].rearrange("p (h k) -> p h k", k=KD),
                             w[heads, c * P:(c + 1) * P, :].rearrange("h p k -> p h k")).then_inc(w_in, 16)
        load(0, 1)
        if not norm:
            sp.wait_ge(projected_before, STEPS + START)
        for c in range(DC):
            sp.dma_start(wq[:, c, :].rearrange("p (h k) -> p h k", k=KD),
                         Wq[heads, c * P:(c + 1) * P, :].rearrange("h p k -> p h k")).then_inc(wqo_in, 16)
        Wo_v = Wo[heads, :, :].rearrange("(a e) k d -> e k a d", e=2)
        for e in range(2):
            sp.dma_start(wo[e * KD:(e + 1) * KD, :, :], Wo_v[e]).then_inc(wqo_in, 16)
        with sp.Fori(0, NC // 2 - 1) as i:
            for b in range(2):
                if norm:
                    sp.wait_ge(x_transposed, i * 2 + b + 1)
                else:
                    sp.wait_ge(v_proj, i * 4 + (2 * b + 2 + START))
                load(i + 1, b)

        if norm:
            for b in range(2):
                sp.wait_ge(h_out[b], 16 * (NC // 2 + START))
        load_hq(0)
        sp.sem_inc(rden_stored, 16 * START)

        def step(i, h, nxt, nxt2, prev):
            sp.wait_ge(late_transposed, count(i, h, QT, QT))
            for qi in range(QUAD):
                for qj in range(QUAD):
                    if qi != qj:
                        src, dst = late_blocks(h, qi, qj)
                        sp.dma_start(dst, src).then_inc(late_moved, 16)
            sp.wait_ge(den_ready, count(i, h, 1, 1))
            sp.dma_start(rden_scratch[h % 2], rden[:, :]).then_inc(rden_stored, 16)
            sp.wait_ge(rden_stored, count(i, h, 16, 16 + 16 * START))
            sp.wait_ge(o_ready, count(i, h, 1, START))
            sp.dma_start(RB[:, :], rden_scratch[h % 2].rearrange("p q -> (p q)").partition_broadcast(KD)).then_inc(rden_in, 16)
            more = not (isinstance(i, int) and i == PAIRS - 1)
            if h == 1 and more:
                sp.wait_ge(q_proj, count(i, 4, 1, 0))
                load_hq(i + 1)

        steps(sp, step)

    def gpsimd_program(pool):
        def load_adj(i, q, first):
            for k in range(SPT):
                if first and not norm:
                    pool.wait_ge(slot_masked_before, SLOTS * STEPS + q * SPT + k + 1 - SLOTS)
                if not first:
                    pool.wait_ge(slot_masked, count(i, 0, SLOTS, q * SPT + k + 1 - SLOTS))
                rows = adj[bass.ds(i * QW + q * P, P), k * SLOT:(k + 1) * SLOT]
                pool.dma_start(B[:, q, k * SLOT:(k + 1) * SLOT], rows).then_inc(adj_in[q][k], 16)

        def convert(i, q):
            for k in range(SPT):
                wait_apart(pool, adj_in[q][k], i * 16 + 16, pool_passed)
                part = B[:, q, k * SLOT:(k + 1) * SLOT]
                last = nc.gpsimd.tensor_scalar(part, part, -1.0, MASK_VAL / SCALE, ALU.add, ALU.mult)
            last.then_inc(bias_conv, 1)
            pool.wait_ge(bias_conv, i * QT + q + 1)
            own = B[:, q, bass.ds(i * QW + q * P, P)]
            nc.gpsimd.tensor_tensor(own, own, notI[:, :], ALU.mult).then_inc(bias_ready, 1)

        def load_base(i):
            pool.dma_start(acc[:, :, :], base[bass.ds(i * QW, QW), :].rearrange("(a p) d -> p a d", p=P)).then_inc(base_in, 16)

        def store(i):
            pool.wait_ge(head_added, count(i, GROUP - 1, 1, 1 + START))
            pool.dma_start(result[bass.ds(i * QW, QW), :].rearrange("(a p) d -> p a d", p=P), res[:, :, :]).then_inc(stored, 16)

        def inverse_deviation(i, b):
            pool.wait_ge(var_ready, i * 2 + (b + 1))
            nc.gpsimd.tensor_tensor(rstd[:, b, :], mv[:, b, :, 1], half[:, :], ALU.pow).then_inc(rstd_ready, 1)

        if norm:
            pool.wait_ge(half_set, 1)
            inverse_deviation(0, 0)
            inverse_deviation(0, 1)
        for q in range(QT):
            load_adj(0, q, True)
        if norm:
            with pool.Fori(1, NC // 2) as i:
                for b in range(2):
                    inverse_deviation(i, b)
        for q in range(QT):
            convert(0, q)
        load_base(0)
        with pool.Fori(1, PAIRS) as i:
            for q in range(QT):
                load_adj(i, q, False)
                convert(i, q)
            store(i - 1)
            pool.wait_ge(stored, i * 16)
            load_base(i)
        store(PAIRS - 1)
        pool.wait_ge(stored, 16 * PAIRS)

    def tensor_program(pe):
        def transpose_x(i, b):
            pe.wait_ge(normed, i * 2 + (b + 1))
            pe.wait_ge(h_ready, i * 2 + (b + START))
            for c in range(DC):
                for r in range(CR):
                    last = nc.tensor.transpose(psT[c][:, r * P:(r + 1) * P], xb[b][:, r, c * P:(c + 1) * P], ident[:, :])
            last.then_inc(x_transposed, 1)

        def keys_values(i, b, nxt, nxt2):
            if norm:
                pe.wait_ge(h_ready, i * 2 + (b + 1 + START))
            else:
                pe.wait_ge(h_in[b], i * 16 + 16)
            for pair in range(GROUP // 2):
                if not norm:
                    pe.wait_ge(slot_masked_before, SLOTS * STEPS)
                pe.wait_ge(k_lo, i * (2 * GROUP) + (b * GROUP + 2 * (pair + 1)))
                for c in range(DC):
                    last = nc.tensor.matmul(psK[pair][b], wk[:, c, pair * P:(pair + 1) * P], hc[b][:, c, :],
                                            start=(c == 0), stop=(c == DC - 1))
                last.then_inc(k_proj, 1)
            if norm and nxt:
                transpose_x(*after(i, b))
            for u, read in ((0, v_act), (1, v_dve)):
                if not norm:
                    pe.wait_ge(o_summed_before if u == 0 else head_added_before, STEPS + START)
                pe.wait_ge(read, i * 2 + (b + START))
                for a in range(2):
                    m = 2 * u + a
                    for c in range(DC):
                        last = nc.tensor.matmul(psV[u][:, a * 256:(a + 1) * 256], hc[b][:, c, m * P:(m + 1) * P],
                                                wv[:, c, :], start=(c == 0), stop=(c == DC - 1))
                last.then_inc(v_proj, 1)

        def query(i, h, wait_hq, first):
            if wait_hq:
                pe.wait_ge(hq_in, i * 16 + 16)
            pe.wait_ge(q_lo, count(i, h, 1, 0))
            if not first:
                pe.wait_ge(head_added, count(i, h, 1, START - 2))
            for c in range(DC):
                last = nc.tensor.matmul(psP[:, 0:QW], wq[:, c, h * KD:(h + 2) * KD], hq[:, c, :],
                                        start=(c == 0), stop=(c == DC - 1))
            last.then_inc(q_proj, 2)

        def scores(i, h, j, first=False):
            q, k = divmod(j, SPT)
            if j == 0:
                pe.wait_ge(q_hi, count(i, h, 1, 1))
                pe.wait_ge(q_lo, count(i, h, 1, 1))
            if not (first and j < 2):
                pe.wait_ge(slot_masked, count(i, h, SLOTS, j - 1))
            for part, hi in ((QH, True), (QL, False)):
                for b in range(SLOT // BANK):
                    col = k * SLOT + b * BANK
                    last = nc.tensor.matmul(psS[j % 2][:, b * BANK:(b + 1) * BANK], part[:, h, q * P:(q + 1) * P],
                                            K2[:, h, col:col + BANK], start=hi, stop=not hi)
            last.then_inc(scores_ready, 1)

        def transposes(i, h, s):
            if s % 4 == 0:
                pe.wait_ge(probs_ready, count(i, h, SLOTS, SPT + s // 4 + 2))
            pe.wait_ge(pt_dve if s % 2 else pt_act, count(i, h, TS // 2, s // 2 + START))
            for a in range(2):
                for q in range(QT):
                    col = (2 * s + a) * P
                    last = nc.tensor.transpose(psT[s % 2][:, a * QW + q * P:a * QW + (q + 1) * P],
                                               S[:, h % 2, q, col:col + P], ident[:, :])
            last.then_inc(transposed, 1)

        def values(i, h, s):
            pe.wait_ge(pt_dve if s % 2 else pt_act, count(i, h, TS // 2, s // 2 + 1 + START))
            if s == 0:
                pe.wait_ge(o_summed, count(i, h, 1, START))
            for a in range(2):
                last = nc.tensor.matmul(psO[a * KD:(a + 1) * KD, 0:QW], V[:, 2 * s + a, h * KD:(h + 1) * KD],
                                        PT[:, s % RING, a * QW:(a + 1) * QW], start=(s == 0), stop=False)
            last.then_inc(pt_free, 1)

        def values_late(i, h):
            pe.wait_ge(late_moved, count(i, h, 16 * MOVES, 16 * MOVES))
            pe.wait_ge(late_copied, count(i, h, QUAD, QUAD))
            PTL = S[:, h % 2, :, LC:N].rearrange("p q (i m a) -> p m q i a", i=QUAD, a=32)
            for m in range(LATE):
                half_ = m % 2
                last = nc.tensor.matmul(psO[half_ * KD:(half_ + 1) * KD, 0:QW], V[:, MT - LATE + m, h * KD:(h + 1) * KD],
                                        PTL[:, m, :, :, :], start=False, stop=(m >= LATE - 2))
            last.then_inc(late_used, 1)

        def project(i, h):
            pe.wait_ge(o_ready, count(i, h, 1, 1 + START))
            pe.wait_ge(head_added, count(i, h, 1, START - 1))
            for q in range(QT):
                last = nc.tensor.matmul(psP[:, q * D:(q + 1) * D], O[:, q * P:(q + 1) * P], wo[:, h // 2, :], start=True, stop=True)
            last.then_inc(projected, 2)

        def step(i, h, nxt, nxt2, prev):
            i1, h1 = (i, h + 1) if h + 1 < GROUP else (i + 1, 0)
            i2, h2 = (i, h + 2) if h + 2 < GROUP else (i + 1, h + 2 - GROUP)
            for c in range(SUBSTEPS):
                transposes(i, h, 2 * c)
                if nxt:
                    scores(i1, h1, c + 2)
                if prev and h % 2 == 0 and c == PROJECT_AT:
                    pe.wait_ge(q_lo, count(i, h, 1, 2))
                    project(*last_step(i, h))
                if c:
                    values(i, h, 2 * c - 2)
                transposes(i, h, 2 * c + 1)
                if c:
                    values(i, h, 2 * c - 1)
                if nxt2 and h % 2 == 0 and c == QUERY_AT:
                    query(i2, h2, h2 == 0, False)
            values(i, h, TS - 2)
            if nxt2:
                scores(i2, h2, 0)
            values(i, h, TS - 1)
            values_late(i, h)
            if nxt2:
                scores(i2, h2, 1)

        pe.sem_inc(v_proj, START)
        pe.wait_ge(w_in, 16 * 2 * DC)
        if norm:
            transpose_x(0, 0)
        chunks(pe, keys_values)

        pe.sem_inc(pt_free, RING)
        pe.sem_inc(projected, START)
        pe.wait_ge(wqo_in, 16 * (DC + 2))
        pe.wait_ge(k_lo, NC * GROUP + 2 * GROUP)
        pe.wait_ge(v_act, NC + START)
        pe.wait_ge(v_dve, NC + START)
        query(0, 0, True, True)
        for j in range(SLOTS):
            scores(0, 0, j, True)
        scores(0, 1, 0)
        scores(0, 1, 1)
        steps(pe, step)
        project(PAIRS - 1, GROUP - 1)

    def scalar_program(act):
        def relu(i, b):
            act.wait_ge(x_transposed, i * 2 + (b + 1))
            if not (isinstance(i, int) and i == b == 0):
                act.wait_ge(v_proj, i * 4 + (2 * b - 2 + START))
            act.wait_ge(h_out[b], i * 16 + 16 * START)
            for c in range(DC):
                last = nc.scalar.activation(hc[b][:, c, :], psT[c][:, :], ACT.Relu)
            last.then_inc(h_ready, 1)
            act.wait_ge(h_ready, i * 2 + (b + 1 + START))
            act.dma_start(hT[:, :, bass.ds((i * 2 + b) * CH, CH)], hc[b]).then_inc(h_out[b], 16)

        def keys_values(i, b, nxt, nxt2):
            for h in range(GROUP):
                act.wait_ge(k_proj, i * GROUP + (b * (GROUP // 2) + h // 2 + 1))
                rows = slice(h % 2 * KD, (h % 2 + 1) * KD)
                nc.scalar.activation(K2[0:KD, h, bass.ds((i * 2 + b) * CH, CH)], psK[h // 2][b][rows, :], ACT.Copy).then_inc(k_hi, 1)
            if norm and nxt:
                relu(*after(i, b))
            act.wait_ge(v_proj, i * 4 + (2 * b + 1 + START))
            nc.scalar.activation(V[:, bass.ds((i * 2 + b) * CR, 2), :], psV[0][:, :].rearrange("p (a n) -> p a n", a=2),
                                 ACT.Copy).then_inc(v_act, 1)

        def query_hi(i, h):
            act.wait_ge(q_proj, count(i, h, 1, 2))
            for e in range(2):
                for half_ in range(2):
                    last = nc.scalar.activation(QH[half_ * KD:(half_ + 1) * KD, h + e, :], psP[e * KD:(e + 1) * KD, 0:QW], ACT.Copy)
            last.then_inc(q_hi, 2)

        def exps(i, h, q, k):
            if k == EXP_ORDER[0]:
                act.wait_ge(row_ready, count(i, h, QT, q + 1))
            part = S[:, h % 2, q, k * SLOT:(k + 1) * SLOT]
            nc.scalar.activation(part, part, ACT.Exp, bias=negm[:, h % 2, q:q + 1],
                                 accum_out=sums[:, h % 2, q, k:k + 1]).then_inc(probs_ready, 1)

        def copy_late(i, h):
            act.wait_ge(late_transposed, count(i, h, QT, QT))
            for qi in range(QUAD):
                src, dst = late_blocks(h, qi, qi)
                nc.scalar.activation(dst, src, ACT.Copy).then_inc(late_copied, 1)

        def step(i, h, nxt, nxt2, prev):
            i1, h1 = (i, h + 1) if h + 1 < GROUP else (i + 1, 0)
            i2, h2 = (i, h + 2) if h + 2 < GROUP else (i + 1, h + 2 - GROUP)
            for c in range(SUBSTEPS):
                s = 2 * c
                act.wait_ge(transposed, count(i, h, TS, s + 1))
                act.wait_ge(pt_free, count(i, h, TS, s + 1))
                nc.scalar.activation(PT[:, s % RING, :], psT[0][:, :], ACT.Copy).then_inc(pt_act, 1)
                if c in (0, 2):
                    exps(i, h, 1, c // 2 + 1)
                if c == 1:
                    copy_late(i, h)
                if nxt and c >= SUBSTEPS - 3:
                    exps(i1, h1, 0, EXP_ORDER[c - (SUBSTEPS - 3)])
                if nxt2 and h % 2 == 0 and c == QUERY_AT:
                    act.wait_ge(scores_ready, count(i, h, SLOTS, SLOTS))
                    query_hi(i2, h2)
            if nxt:
                exps(i1, h1, 0, EXP_ORDER[SPT - 1])
                exps(i1, h1, 1, EXP_ORDER[0])
            if nxt:
                exps(i1, h1, 1, 0)
            act.wait_ge(late_used, count(i, h, 1, 1))
            act.wait_ge(o_ready, count(i, h, 1, START))
            nc.scalar.activation(Oodd[:, :], psO[KD:2 * KD, 0:QW], ACT.Copy).then_inc(odd_copied, 1)

        act.sem_inc(v_act, START)
        if norm:
            act.sem_inc(h_ready, START)
            for b in range(2):
                act.sem_inc(h_out[b], 16 * START)
            relu(0, 0)
        chunks(act, keys_values)

        act.sem_inc(pt_act, START)
        query_hi(0, 0)
        for k in EXP_ORDER:
            exps(0, 0, 0, k)
        for k in EXP_ORDER[:2]:
            exps(0, 0, 1, k)
        steps(act, step)

    def vector_program(dve):
        def statistics(i, b):
            dve.wait_ge(x_in[b], i * 16 + 16)
            for r in range(CR):
                nc.vector.bn_stats(stats[:, b, r, :], xb[b][:, r, :]).then_inc(stat1, 1)
            wait_apart(dve, stat1, i * (2 * CR) + (b + 1) * CR, dve_passed)
            for r in range(CR):
                nc.vector.bn_aggr(mv[:, b, r, :], stats[:, b, r, :]).then_inc(aggr, 1)
            dve.wait_ge(aggr, i * (2 * CR) + (b + 1) * CR)
            nc.vector.tensor_scalar(mv[:, b, :, 1], mv[:, b, :, 1], EPS, None, ALU.add).then_inc(var_ready, 1)

        def normalise(i, b):
            dve.wait_ge(rstd_ready, i * 2 + (b + 1))
            for r in range(CR):
                last = nc.vector.tensor_scalar(xb[b][:, r, :], xb[b][:, r, :], mv[:, b, r, 0:1],
                                               rstd[:, b, r:r + 1], ALU.subtract, ALU.mult)
            last.then_inc(normed, 1)

        def keys_values(i, b, nxt, nxt2):
            if norm and nxt:
                normalise(*after(i, b))
            for h in range(GROUP):
                if h == 2 and norm and nxt2:
                    statistics(i + 1, b)
                dve.wait_ge(k_hi, i * (2 * GROUP) + (b * GROUP + h + 1))
                rows = slice(h % 2 * KD, (h % 2 + 1) * KD)
                cols = bass.ds((i * 2 + b) * CH, CH)
                nc.vector.tensor_tensor(K2[KD:2 * KD, h, cols], psK[h // 2][b][rows, :], K2.bitcast(F32)[0:KD, h, cols],
                                        ALU.subtract).then_inc(k_lo, 1)
            dve.wait_ge(v_proj, i * 4 + (2 * b + 2 + START))
            nc.vector.tensor_copy(V[:, bass.ds((i * 2 + b) * CR + 2, 2), :],
                                  psV[1][:, :].rearrange("p (a n) -> p a n", a=2)).then_inc(v_dve, 1)

        def query_lo(i, h):
            dve.wait_ge(q_hi, count(i, h, 1, 2))
            for e in range(2):
                for half_ in range(2):
                    rows = slice(half_ * KD, (half_ + 1) * KD)
                    last = nc.vector.tensor_tensor(QL[rows, h + e, :], psP[e * KD:(e + 1) * KD, 0:QW],
                                                   QH.bitcast(F32)[rows, h + e, :], ALU.subtract)
            last.then_inc(q_lo, 2)

        def mask(i, h, j, first=False):
            q, k = divmod(j, SPT)
            if h == 0 and k == 0:
                dve.wait_ge(bias_ready, i * QT + (q + 1))
            if j == SPT + 1 and not first:
                dve.wait_ge(late_moved, count(i, h, 16 * MOVES, 0))
                dve.wait_ge(late_copied, count(i, h, QUAD, 0))
            wait_apart(dve, scores_ready, count(i, h, SLOTS, j + 1), dve_passed)
            part = S[:, h % 2, q, k * SLOT:(k + 1) * SLOT]
            nc.vector.tensor_tensor_reduce(out=part, in0=psS[j % 2][:, :], in1=B[:, q, k * SLOT:(k + 1) * SLOT],
                                           scale=SCALE, scalar=LOWEST, op0=ALU.add, op1=ALU.max,
                                           accum_out=mx[:, h % 2, q, k:k + 1]).then_inc(slot_masked, 1)
            if k == SPT - 1:
                dve.wait_ge(slot_masked, count(i, h, SLOTS, j + 1))
                own = S[:, h % 2, q, bass.ds(i * QW + q * P, P)]
                nc.vector.tensor_tensor(own, own, diag[:, :], ALU.add)
                nc.vector.tensor_reduce(negm[:, h % 2, q:q + 1], mx[:, h % 2, q, :], AX_X, ALU.max,
                                        negate=True).then_inc(row_ready, 1)

        def transpose_late(i, h, q, before):
            dve.wait_ge(probs_ready, count(i, h, SLOTS, q * SPT + 1))
            if before:
                dve.wait_ge(transposed, count(i, h, TS, (q + 2) * SLOT // (2 * P) - TS))
            src = S[:, h % 2, q, LC:N].rearrange("p (n b) -> p n b", b=32)
            dst = T1(h)[:, q, :].rearrange("p (j m a) -> p m j a", j=QUAD, a=32)
            nc.vector.transpose(dst, src).then_inc(late_transposed, 1)

        def denominators(i, h):
            dve.wait_ge(probs_ready, count(i, h, SLOTS, SLOTS))
            nc.vector.tensor_reduce(den[:, :], sums[:, h % 2, :, :], AX_X, ALU.add).then_inc(summed, 1)
            dve.wait_ge(summed, count(i, h, 1, 1))
            dve.wait_ge(rden_stored, count(i, h, 16, 16 * START))
            nc.vector.reciprocal(rden[:, :], den[:, :]).then_inc(den_ready, 1)

        def sum_halves(i, h):
            dve.wait_ge(odd_copied, count(i, h, 1, 1))
            nc.vector.tensor_tensor(Oodd[:, :], psO[0:KD, 0:QW], Oodd[:, :], ALU.add).then_inc(o_summed, 1)
            dve.wait_ge(o_summed, count(i, h, 1, 1 + START))
            dve.wait_ge(rden_in, count(i, h, 16, 16))
            dve.wait_ge(projected, count(i, h, 1, START - h % 2))
            half_ = h % 2
            nc.vector.tensor_tensor(O[half_ * KD:(half_ + 1) * KD, :].rearrange("k (q p) -> k q p", q=QT),
                                    Oodd[:, :].rearrange("k (q p) -> k q p", q=QT),
                                    RB[:, :].rearrange("k (p q) -> k q p", q=QT), ALU.mult).then_inc(o_ready, 1)

        def add_heads(i, h):
            dve.wait_ge(projected, count(i, h, 1, 1 + START))
            if h == 1:
                dve.wait_ge(base_in, i * 16 + 16)
            else:
                dve.wait_ge(head_added, count(i, h, 1, START - 1))
            dst = res if h == GROUP - 1 else acc
            nc.vector.tensor_tensor(dst[:, :, :], psP[:, :].rearrange("p (q d) -> p q d", q=QT), acc[:, :, :],
                                    ALU.add).then_inc(head_added, 2)

        def step(i, h, nxt, nxt2, prev):
            i1, h1 = (i, h + 1) if h + 1 < GROUP else (i + 1, 0)
            i2, h2 = (i, h + 2) if h + 2 < GROUP else (i + 1, h + 2 - GROUP)
            for c in range(SUBSTEPS):
                if nxt and c:
                    mask(i1, h1, c + 1)
                if prev and h % 2 == 0 and c == PROJECT_AT + 1:
                    add_heads(*last_step(i, h))
                s = 2 * c + 1
                dve.wait_ge(transposed, count(i, h, TS, s + 1))
                dve.wait_ge(pt_free, count(i, h, TS, s + 1))
                nc.vector.tensor_copy(PT[:, s % RING, :], psT[1][:, :]).then_inc(pt_dve, 1)
                if c == QUERY_AT:
                    denominators(i, h)
                if nxt2 and h % 2 == 0 and c == QUERY_AT + 1:
                    query_lo(i2, h2)
            if nxt:
                mask(i1, h1, SLOTS - 1)
                transpose_late(i1, h1, 0, True)
            if nxt2:
                mask(i2, h2, 0)
            if nxt:
                transpose_late(i1, h1, 1, True)
            if nxt2:
                mask(i2, h2, 1)
            sum_halves(i, h)

        dve.sem_inc(k_lo, 2 * GROUP)
        dve.sem_inc(v_dve, START)
        if norm:
            nc.vector.memset(half[:, :], -0.5).then_inc(half_set, 1)
            statistics(0, 0)
            normalise(0, 0)
            statistics(0, 1)
        chunks(dve, keys_values)

        dve.sem_inc(pt_dve, START)
        dve.sem_inc(head_added, START)
        dve.sem_inc(o_summed, START)
        dve.sem_inc(o_ready, START)
        if norm:
            for b in range(2):
                dve.wait_ge(h_out[b], 16 * (NC // 2 + START))
        query_lo(0, 0)
        for j in range(SLOTS):
            mask(0, 0, j, first=True)
        for q in range(QT):
            transpose_late(0, 0, q, False)
        mask(0, 1, 0)
        mask(0, 1, 1)
        steps(dve, step)
        add_heads(PAIRS - 1, GROUP - 1)

    return ((sync_program, gpsimd_program, tensor_program, scalar_program, vector_program),
            (late_used, slot_masked, projected, o_summed, head_added))


def build(nc, x, adj, Wk, Wq, Wv, Wo, out):
    hT = nc.dram_tensor("hT_scratch", [P, DC, N], F32, kind="Internal").ap()
    rden_scratch = nc.dram_tensor("rden_scratch", [2, P, QT], F32, kind="Internal").ap()
    partial = nc.dram_tensor("partial_scratch", [N, D], F32, kind="Internal").ap()
    with ExitStack() as ctx:
        def sb(name, shape, dt=F32):
            return ctx.enter_context(nc.sbuf_tensor(name, shape, dt))

        def sem(name):
            return ctx.enter_context(nc.semaphore(name))

        K2 = sb("K2", [P, GROUP, N], F32R)
        V = sb("V", [P, MT, GROUP * KD])
        S = sb("S", [P, 2, QT, N])
        B = sb("B", [P, QT, N], BF16)
        PT = sb("PT", [P, RING, 2 * QW])
        QH = sb("QH", [P, GROUP, QW], F32R)
        QL = sb("QL", [P, GROUP, QW], F32R)
        hq = sb("hq", [P, DC, QW])
        wq = sb("wq", [P, DC, GROUP * KD])
        wo = sb("wo", [P, GROUP // 2, D])
        O = sb("O", [P, QW])
        Oodd = sb("Oodd", [KD, QW])
        RB = sb("RB", [KD, QW])
        acc = sb("acc", [P, QT, D])
        res = sb("res", [P, QT, D])
        ident = sb("ident", [P, P])
        notI = sb("notI", [P, P], BF16)
        diag = sb("diag", [P, P])
        mx = sb("mx", [P, 2, QT, SPT])
        negm = sb("negm", [P, 2, QT])
        sums = sb("sums", [P, 2, QT, SPT])
        den = sb("den", [P, QT])
        rden = sb("rden", [P, QT])
        stats = sb("stats", [P, 2, CR, 6])
        mv = sb("mv", [P, 2, CR, 2])
        rstd = sb("rstd", [P, 2, CR])
        half = sb("half", [P, CR])
        psS = [ctx.enter_context(nc.psum_tensor(f"psS{j}", [P, SLOT], F32)) for j in range(2)]
        psT = [ctx.enter_context(nc.psum_tensor(f"psT{j}", [P, BANK], F32)) for j in range(2)]
        psO = ctx.enter_context(nc.psum_tensor("psO", [P, BANK], F32))
        psP = ctx.enter_context(nc.psum_tensor("psP", [P, BANK], F32))

        xb = [S[:, 1, 0, b * 1024:(b + 1) * 1024].rearrange("p (r d) -> p r d", d=D) for b in range(2)]
        hc = [S[:, 0, 0, b * 1024:(b + 1) * 1024].rearrange("p (c n) -> p c n", c=DC) for b in range(2)]
        wk = S[:, 0, 1, 0:512].rearrange("p (c n) -> p c n", c=DC)
        wv = S[:, 0, 1, 512:1024].rearrange("p (c n) -> p c n", c=DC)

        ones_set, consts = sem("ones_set"), sem("consts")
        with nc.Block() as block:
            @block.gpsimd
            def _(pool):
                nc.gpsimd.memset(ident[:, :], 0.0).then_inc(ones_set, 1)
                nc.gpsimd.memset(notI[:, :], 1.0).then_inc(ones_set, 1)
                nc.gpsimd.memset(diag[:, :], 0.0).then_inc(ones_set, 1)
                pool.wait_ge(ones_set, 3)
                for m, fill in ((ident, 1.0), (notI, 0.0), (diag, IDENTITY_BIAS)):
                    nc.gpsimd.affine_select(out=m[:, :], in_=m[:, :], compare_op=ALU.not_equal, fill=fill, base=0,
                                            pattern=[[-1, P]], channel_multiplier=1).then_inc(consts, 1)
                pool.wait_ge(consts, 3)

        tiles = (K2, V, S, B, PT, QH, QL, hq, wq, wo, O, Oodd, RB, acc, res, ident, notI, diag, mx, negm, sums, den, rden,
                 stats, mv, rstd, half, xb, hc, wk, wv, psS, psT, psO, psP, rden_scratch)
        programs, before = [], None
        for g in range(GROUPS):
            program, before = group_programs(nc, sem, g, before, x, hT, adj, Wk, Wq, Wv, Wo, x if g == 0 else partial,
                                             out if g == GROUPS - 1 else partial, tiles)
            programs.append(program)
        with nc.Block() as block:
            @block.sync
            def _(sp):
                for sync_program, _, _, _, _ in programs:
                    sync_program(sp)

            @block.gpsimd
            def _(pool):
                for _, gpsimd_program, _, _, _ in programs:
                    gpsimd_program(pool)

            @block.tensor
            def _(pe):
                for _, _, tensor_program, _, _ in programs:
                    tensor_program(pe)

            @block.scalar
            def _(act):
                for _, _, _, scalar_program, _ in programs:
                    scalar_program(act)

            @block.vector
            def _(dve):
                for _, _, _, _, vector_program in programs:
                    vector_program(dve)


def kernel(x, adj, L0_gnn_Wks, L0_gnn_Wqs, L0_gnn_Wvs, L0_gnn_Wo):
    import concourse.bacc as bacc
    import numpy as np
    from concourse.bass_utils import run_bass_kernel_spmd

    nc = bacc.Bacc("TRN2", target_bir_lowering=False, num_devices=1)
    arrays, args = {}, []
    for name, a in (("x", x), ("adj", adj), ("Wk", L0_gnn_Wks), ("Wq", L0_gnn_Wqs), ("Wv", L0_gnn_Wvs), ("Wo", L0_gnn_Wo)):
        a = np.ascontiguousarray(a)
        arrays[f"in_{name}"] = a
        args.append(nc.dram_tensor(f"in_{name}", a.shape, mybir.dt.from_np(a.dtype), kind="ExternalInput").ap())
    out = nc.dram_tensor("out", [N, D], F32, kind="ExternalOutput").ap()
    build(nc, *args, out)
    r = run_bass_kernel_spmd(nc, [arrays], core_ids=[0])
    return r.results[0]["out"]
```

```python
from contextlib import ExitStack

import concourse.bass as bass
from concourse import mybir
from concourse.alu_op_type import AluOpType as ALU

ACT = mybir.ActivationFunctionType
AX_X = mybir.AxisListType.X
F32 = mybir.dt.float32
F32R = mybir.dt.float32r
BF16 = mybir.dt.bfloat16

N, D, HEADS, KD = 4096, 256, 8, 64
P = 128
DC = D // P
GROUP = 4
GROUPS = HEADS // GROUP
QT = 2
QW = QT * P
PAIRS = N // QW
STEPS = PAIRS * GROUP
MT = N // P
SLOT = 1024
SPT = N // SLOT
SLOTS = QT * SPT
LATE = 12
LC = N - LATE * P
TS = (MT - LATE) // 2
QUAD = P // 32
MOVES = QUAD * (QUAD - 1)
RING = 4
BANK = 512
CH = 512
CR = CH // P
NC = N // CH
EPS = 1e-5
SCALE = float(KD) ** -0.5
IDENTITY_BIAS = 0.01
MASK_VAL = 1e16
LOWEST = -3.0e38

SUBSTEPS = TS // 2
PIECES = [(LC, N), (0, SLOT), (SLOT, LC)]
NE = len(PIECES)
ACT_SLOTS = [0, 2, 4, 6, 8, 9]
DVE_SLOTS = [1, 3, 5, 7]
PROJECT_AT = 1
QUERY_AT = 2


START = 1
PT_START = 2


def count(i, h, per, extra):
    return i * (GROUP * per) + (h * per + extra)


def ring_used(s):
    if s >= RING:
        return s - RING + 1 + RING
    return [b for b in range(TS) if b % RING == s][-1] + 1 - TS + RING


def wait_apart(engine, sem, value, passed):
    engine.wait_ge(sem, value)
    engine.sem_inc(passed, 1)


def group_programs(nc, sem, g, before, x, hT, adj, Wk, Wq, Wv, Wo, base, result, t):
    (K2, V, S, B, PT, QH, QL, hq, wq, wo, O, Oodd, RB, acc, res, ident, notI, diag, mx, negm, sums, den, rden,
     stats, mv, rstd, half, xb, hc, wk, wv, psS, psT, psO, psP, rden_scratch, ones_set, consts) = t
    norm = g == 0
    heads = slice(g * GROUP, (g + 1) * GROUP)
    x_v = x.rearrange("(n r p) d -> n p r d", p=P, r=CR)
    psK = [[psS[pair][:, b * BANK:(b + 1) * BANK] for b in range(2)] for pair in range(GROUP // 2)]
    psV = [psO, psP]

    x_in = [sem(f"x_in{g}{b}") for b in range(2)]
    h_in = [sem(f"h_in{g}{b}") for b in range(2)]
    h_out = [sem(f"h_out{g}{b}") for b in range(2)]
    (w_in, wqo_in, half_set, stat1, aggr, var_ready, rstd_ready, normed, x_transposed, h_ready, k_proj, v_proj, k_hi, k_lo,
     v_act, v_dve) = (sem(f"{s}{g}") for s in (
         "w_in", "wqo_in", "half_set", "stat1", "aggr", "var_ready", "rstd_ready", "normed", "x_transposed", "h_ready",
         "k_proj", "v_proj", "k_hi", "k_lo", "v_act", "v_dve"))

    hq_in, base_in, stored = sem(f"hq_in{g}"), sem(f"base_in{g}"), sem(f"stored{g}")
    dve_passed, pool_passed = sem(f"dve_passed{g}"), sem(f"pool_passed{g}")
    adj_in = [[sem(f"adj_in{g}{q}{k}") for k in range(SPT)] for q in range(QT)]
    (bias_conv, bias_ready, q_proj, q_hi, q_lo, scores_ready, slot_masked, row_ready, probs_ready,
     transposed, pt_act, pt_dve, pt_free, o_ready, projected, summed, den_ready, head_added,
     late_transposed, late_moved, late_copied, late_used, odd_copied, o_summed, rden_stored, rden_in) = (
        sem(f"{s}{g}") for s in (
            "bias_conv", "bias_ready", "q_proj", "q_hi", "q_lo", "scores_ready", "slot_masked", "row_ready",
            "probs_ready", "transposed", "pt_act", "pt_dve", "pt_free", "o_ready", "projected", "summed", "den_ready",
            "head_added", "late_transposed", "late_moved", "late_copied", "late_used", "odd_copied", "o_summed",
            "rden_stored", "rden_in"))

    def chunks(engine, body):
        with engine.Fori(0, NC // 2 - 1) as i:
            for b in range(2):
                body(i, b, True, True)
        body(NC // 2 - 1, 0, True, False)
        body(NC // 2 - 1, 1, False, False)

    def after(i, b):
        return (i, 1) if b == 0 else (i + 1, 0)

    def query_psum(first):
        return psT[0] if first else psP

    def wait_taken(engine, i, h, s):
        slots, taken, start = (ACT_SLOTS, pt_act, PT_START) if s % TS in ACT_SLOTS else (DVE_SLOTS, pt_dve, 0)
        engine.wait_ge(taken, count(i, h, len(slots), slots.index(s % TS) + 1 + start - (len(slots) if s < 0 else 0)))

    def T1(h):
        return S[:, (h + 1) % 2, 1, N - QT * LATE * P:N].rearrange("p (q n) -> p q n", q=QT)

    def last_step(i, h):
        return (i, h - 1) if h else (i - 1, GROUP - 1)

    def late_blocks(h, qi, qj):
        part = LATE * 32
        return (T1(h)[qi * 32:(qi + 1) * 32, :, qj * part:(qj + 1) * part],
                S[qj * 32:(qj + 1) * 32, h % 2, :, LC + qi * part:LC + (qi + 1) * part])

    def steps(engine, body):
        for h in range(GROUP):
            body(0, h, True, True, h > 0)
        with engine.Fori(1, PAIRS - 1) as i:
            for h in range(GROUP):
                body(i, h, True, True, True)
        for h in range(GROUP):
            body(PAIRS - 1, h, h + 1 < GROUP, h + 2 < GROUP, True)

    if not norm:
        late_used_before, slot_masked_before, projected_before, o_summed_before, head_added_before = before

    def sync_program(sp):
        def load_hq(i):
            sp.dma_start(hq[:, :, :], hT[:, :, bass.ds(i * QW, QW)]).then_inc(hq_in, 16)

        def load_x(i, b):
            sp.dma_start(xb[b], x_v[bass.ds(i * 2 + b, 1), :, :, :].rearrange("a p r d -> p (a r) d")).then_inc(x_in[b], 16)

        def load_h(i, b):
            sp.dma_start(hc[b], hT[:, :, bass.ds((i * 2 + b) * CH, CH)]).then_inc(h_in[b], 16)

        load = load_x if norm else load_h
        if not norm:
            sp.wait_ge(late_used_before, STEPS - 1)
        load(0, 0)
        for w, dst in ((Wk, wk), (Wv, wv)):
            for c in range(DC):
                sp.dma_start(dst[:, c, :].rearrange("p (h k) -> p h k", k=KD),
                             w[heads, c * P:(c + 1) * P, :].rearrange("h p k -> p h k")).then_inc(w_in, 16)
        load(0, 1)
        if not norm:
            sp.wait_ge(projected_before, STEPS + START)
        for c in range(DC):
            sp.dma_start(wq[:, c, :].rearrange("p (h k) -> p h k", k=KD),
                         Wq[heads, c * P:(c + 1) * P, :].rearrange("h p k -> p h k")).then_inc(wqo_in, 16)
        Wo_v = Wo[heads, :, :].rearrange("(a e) k d -> e k a d", e=2)
        for e in range(2):
            sp.dma_start(wo[e * KD:(e + 1) * KD, :, :], Wo_v[e]).then_inc(wqo_in, 16)
        with sp.Fori(0, NC // 2 - 1) as i:
            for b in range(2):
                if norm:
                    sp.wait_ge(x_transposed, i * 2 + b + 1)
                else:
                    sp.wait_ge(v_proj, i * 4 + (2 * b + 2 + START))
                load(i + 1, b)

        if norm:
            sp.wait_ge(h_out[0], 16 * (1 + START))
        load_hq(0)
        if norm:
            for b in range(2):
                sp.wait_ge(h_out[b], 16 * (NC // 2 + START))
        sp.sem_inc(rden_stored, 16 * START)

        def step(i, h, nxt, nxt2, prev):
            sp.wait_ge(late_transposed, count(i, h, QT, QT))
            for qi in range(QUAD):
                for qj in range(QUAD):
                    if qi != qj:
                        src, dst = late_blocks(h, qi, qj)
                        sp.dma_start(dst, src).then_inc(late_moved, 16)
            sp.wait_ge(den_ready, count(i, h, 1, 1))
            sp.dma_start(rden_scratch[h % 2], rden[:, :]).then_inc(rden_stored, 16)
            sp.wait_ge(rden_stored, count(i, h, 16, 16 + 16 * START))
            sp.wait_ge(o_ready, count(i, h, 1, START))
            sp.dma_start(RB[:, :], rden_scratch[h % 2].rearrange("p q -> (p q)").partition_broadcast(KD)).then_inc(rden_in, 16)
            more = not (isinstance(i, int) and i == PAIRS - 1)
            if h == 1 and more:
                sp.wait_ge(q_proj, count(i, 4, 1, 0))
                load_hq(i + 1)

        steps(sp, step)

    def gpsimd_program(pool):
        def load_adj(i, q, first):
            for k in range(SPT):
                if first and not norm:
                    pool.wait_ge(slot_masked_before, SLOTS * STEPS + q * SPT + k + 1 - SLOTS)
                if not first:
                    pool.wait_ge(slot_masked, count(i, 0, SLOTS, q * SPT + k + 1 - SLOTS))
                rows = adj[bass.ds(i * QW + q * P, P), k * SLOT:(k + 1) * SLOT]
                pool.dma_start(B[:, q, k * SLOT:(k + 1) * SLOT], rows).then_inc(adj_in[q][k], 16)

        def convert(i, q):
            for k in range(SPT):
                wait_apart(pool, adj_in[q][k], i * 16 + 16, pool_passed)
                part = B[:, q, k * SLOT:(k + 1) * SLOT]
                last = nc.gpsimd.tensor_scalar(part, part, -1.0, MASK_VAL / SCALE, ALU.add, ALU.mult)
            last.then_inc(bias_conv, 1)
            pool.wait_ge(bias_conv, i * QT + q + 1)
            own = B[:, q, bass.ds(i * QW + q * P, P)]
            nc.gpsimd.tensor_tensor(own, own, notI[:, :], ALU.mult).then_inc(bias_ready, 1)

        def load_base(i):
            pool.dma_start(acc[:, :, :], base[bass.ds(i * QW, QW), :].rearrange("(a p) d -> p a d", p=P)).then_inc(base_in, 16)

        def store(i):
            pool.wait_ge(head_added, count(i, GROUP - 1, 1, 1 + START))
            pool.dma_start(result[bass.ds(i * QW, QW), :].rearrange("(a p) d -> p a d", p=P), res[:, :, :]).then_inc(stored, 16)

        def inverse_deviation(i, b):
            pool.wait_ge(var_ready, i * 2 + (b + 1))
            nc.gpsimd.tensor_tensor(rstd[:, b, :], mv[:, b, :, 1], half[:, :], ALU.pow).then_inc(rstd_ready, 1)

        def constants():
            nc.gpsimd.memset(ident[:, :], 0.0).then_inc(ones_set, 1)
            nc.gpsimd.memset(notI[:, :], 1.0).then_inc(ones_set, 1)
            nc.gpsimd.memset(diag[:, :], 0.0).then_inc(ones_set, 1)
            pool.wait_ge(ones_set, 3)
            for m, fill in ((ident, 1.0), (notI, 0.0), (diag, IDENTITY_BIAS)):
                nc.gpsimd.affine_select(out=m[:, :], in_=m[:, :], compare_op=ALU.not_equal, fill=fill, base=0,
                                        pattern=[[-1, P]], channel_multiplier=1).then_inc(consts, 1)
            pool.wait_ge(consts, 3)

        if norm:
            constants()
            pool.wait_ge(half_set, 1)
            inverse_deviation(0, 0)
            inverse_deviation(0, 1)
        for q in range(QT):
            load_adj(0, q, True)
        if norm:
            with pool.Fori(1, NC // 2) as i:
                for b in range(2):
                    inverse_deviation(i, b)
        for q in range(QT):
            convert(0, q)
        load_base(0)
        with pool.Fori(1, PAIRS) as i:
            for q in range(QT):
                load_adj(i, q, False)
                convert(i, q)
            store(i - 1)
            pool.wait_ge(stored, i * 16)
            load_base(i)
        store(PAIRS - 1)
        pool.wait_ge(stored, 16 * PAIRS)

    def tensor_program(pe):
        def transpose_x(i, b):
            pe.wait_ge(normed, i * 2 + (b + 1))
            pe.wait_ge(h_ready, i * 2 + (b + START))
            for c in range(DC):
                for r in range(CR):
                    last = nc.tensor.transpose(psT[c][:, r * P:(r + 1) * P], xb[b][:, r, c * P:(c + 1) * P], ident[:, :])
            last.then_inc(x_transposed, 1)

        def keys_values(i, b, nxt, nxt2):
            if norm:
                pe.wait_ge(h_ready, i * 2 + (b + 1 + START))
            else:
                pe.wait_ge(h_in[b], i * 16 + 16)
            for pair in range(GROUP // 2):
                if not norm:
                    pe.wait_ge(slot_masked_before, SLOTS * STEPS)
                pe.wait_ge(k_lo, i * (2 * GROUP) + (b * GROUP + 2 * (pair + 1)))
                for c in range(DC):
                    last = nc.tensor.matmul(psK[pair][b], wk[:, c, pair * P:(pair + 1) * P], hc[b][:, c, :],
                                            start=(c == 0), stop=(c == DC - 1))
                last.then_inc(k_proj, 1)
            if norm and nxt:
                transpose_x(*after(i, b))
            if not nxt:
                pe.wait_ge(wqo_in, 16 * (DC + 2))
                query(0, 0, True, True)
            for u, read in ((0, v_act), (1, v_dve)):
                if not norm:
                    pe.wait_ge(o_summed_before if u == 0 else head_added_before, STEPS + START)
                pe.wait_ge(read, i * 2 + (b + START))
                for a in range(2):
                    m = 2 * u + a
                    for c in range(DC):
                        last = nc.tensor.matmul(psV[u][:, a * 256:(a + 1) * 256], hc[b][:, c, m * P:(m + 1) * P],
                                                wv[:, c, :], start=(c == 0), stop=(c == DC - 1))
                last.then_inc(v_proj, 1)

        def query(i, h, wait_hq, first):
            if wait_hq:
                pe.wait_ge(hq_in, i * 16 + 16)
            pe.wait_ge(q_lo, count(i, h, 1, 0))
            if not first:
                pe.wait_ge(head_added, count(i, h, 1, START - 2))
            for c in range(DC):
                last = nc.tensor.matmul(query_psum(first)[:, 0:QW], wq[:, c, h * KD:(h + 2) * KD], hq[:, c, :],
                                        start=(c == 0), stop=(c == DC - 1))
            last.then_inc(q_proj, 2)

        def scores(i, h, j, first=False):
            q, k = divmod(j, SPT)
            if j == 0:
                pe.wait_ge(q_hi, count(i, h, 1, 1))
                pe.wait_ge(q_lo, count(i, h, 1, 1))
            if not (first and j < 2):
                pe.wait_ge(slot_masked, count(i, h, SLOTS, j - 1))
            for part, hi in ((QH, True), (QL, False)):
                for b in range(SLOT // BANK):
                    col = k * SLOT + b * BANK
                    last = nc.tensor.matmul(psS[j % 2][:, b * BANK:(b + 1) * BANK], part[:, h, q * P:(q + 1) * P],
                                            K2[:, h, col:col + BANK], start=hi, stop=not hi)
            last.then_inc(scores_ready, 1)

        def transposes(i, h, s):
            for e, (first_key, _) in enumerate(PIECES):
                if first_key == 2 * s * P:
                    pe.wait_ge(probs_ready, count(i, h, QT * NE, NE + e + 1))
            wait_taken(pe, i, h, s - 2)
            for a in range(2):
                for q in range(QT):
                    col = (2 * s + a) * P
                    last = nc.tensor.transpose(psT[s % 2][:, a * QW + q * P:a * QW + (q + 1) * P],
                                               S[:, h % 2, q, col:col + P], ident[:, :])
            last.then_inc(transposed, 1)

        def values(i, h, s):
            wait_taken(pe, i, h, s)
            if s == 0:
                pe.wait_ge(o_summed, count(i, h, 1, START))
            for a in range(2):
                last = nc.tensor.matmul(psO[a * KD:(a + 1) * KD, 0:QW], V[:, 2 * s + a, h * KD:(h + 1) * KD],
                                        PT[:, s % RING, a * QW:(a + 1) * QW], start=(s == 0), stop=False)
            last.then_inc(pt_free, 1)

        def values_late(i, h):
            pe.wait_ge(late_moved, count(i, h, 16 * MOVES, 16 * MOVES))
            pe.wait_ge(late_copied, count(i, h, QUAD, QUAD))
            PTL = S[:, h % 2, :, LC:N].rearrange("p q (i m a) -> p m q i a", i=QUAD, a=32)
            for m in range(LATE):
                half_ = m % 2
                last = nc.tensor.matmul(psO[half_ * KD:(half_ + 1) * KD, 0:QW], V[:, MT - LATE + m, h * KD:(h + 1) * KD],
                                        PTL[:, m, :, :, :], start=False, stop=(m >= LATE - 2))
            last.then_inc(late_used, 1)

        def project(i, h):
            pe.wait_ge(o_ready, count(i, h, 1, 1 + START))
            pe.wait_ge(head_added, count(i, h, 1, START - 1))
            for q in range(QT):
                last = nc.tensor.matmul(psP[:, q * D:(q + 1) * D], O[:, q * P:(q + 1) * P], wo[:, h // 2, :], start=True, stop=True)
            last.then_inc(projected, 2)

        def step(i, h, nxt, nxt2, prev):
            i1, h1 = (i, h + 1) if h + 1 < GROUP else (i + 1, 0)
            i2, h2 = (i, h + 2) if h + 2 < GROUP else (i + 1, h + 2 - GROUP)
            for c in range(SUBSTEPS):
                transposes(i, h, 2 * c)
                if nxt:
                    scores(i1, h1, c + 2)
                if prev and h % 2 == 0 and c == PROJECT_AT:
                    pe.wait_ge(q_lo, count(i, h, 1, 2))
                    project(*last_step(i, h))
                if c:
                    values(i, h, 2 * c - 2)
                transposes(i, h, 2 * c + 1)
                if c:
                    values(i, h, 2 * c - 1)
                if nxt2 and h % 2 == 0 and c == QUERY_AT:
                    query(i2, h2, h2 == 0, False)
            if nxt:
                scores(i1, h1, SLOTS - 1)
            values(i, h, TS - 2)
            if nxt2:
                scores(i2, h2, 0)
            values(i, h, TS - 1)
            values_late(i, h)
            if nxt2:
                scores(i2, h2, 1)

        pe.sem_inc(v_proj, START)
        pe.wait_ge(w_in, 16 * 2 * DC)
        if norm:
            pe.wait_ge(consts, 3)
            transpose_x(0, 0)
        chunks(pe, keys_values)

        pe.sem_inc(pt_free, RING)
        pe.sem_inc(projected, START)
        pe.wait_ge(k_lo, NC * GROUP + 2 * GROUP)
        pe.wait_ge(v_act, NC + START)
        pe.wait_ge(v_dve, NC + START)
        for j in range(SLOTS):
            scores(0, 0, j, True)
        scores(0, 1, 0)
        scores(0, 1, 1)
        steps(pe, step)
        project(PAIRS - 1, GROUP - 1)

    def scalar_program(act):
        def relu(i, b):
            act.wait_ge(x_transposed, i * 2 + (b + 1))
            if not (isinstance(i, int) and i == b == 0):
                act.wait_ge(v_proj, i * 4 + (2 * b - 2 + START))
            act.wait_ge(h_out[b], i * 16 + 16 * START)
            for c in range(DC):
                last = nc.scalar.activation(hc[b][:, c, :], psT[c][:, :], ACT.Relu)
            last.then_inc(h_ready, 1)
            act.wait_ge(h_ready, i * 2 + (b + 1 + START))
            act.dma_start(hT[:, :, bass.ds((i * 2 + b) * CH, CH)], hc[b]).then_inc(h_out[b], 16)

        def keys_values(i, b, nxt, nxt2):
            for h in range(GROUP):
                act.wait_ge(k_proj, i * GROUP + (b * (GROUP // 2) + h // 2 + 1))
                rows = slice(h % 2 * KD, (h % 2 + 1) * KD)
                nc.scalar.activation(K2[0:KD, h, bass.ds((i * 2 + b) * CH, CH)], psK[h // 2][b][rows, :], ACT.Copy).then_inc(k_hi, 1)
            if norm and nxt:
                relu(*after(i, b))
            if not nxt:
                query_hi(0, 0, True)
            act.wait_ge(v_proj, i * 4 + (2 * b + 1 + START))
            nc.scalar.activation(V[:, bass.ds((i * 2 + b) * CR, 2), :], psV[0][:, :].rearrange("p (a n) -> p a n", a=2),
                                 ACT.Copy).then_inc(v_act, 1)

        def query_hi(i, h, first=False):
            act.wait_ge(q_proj, count(i, h, 1, 2))
            for e in range(2):
                for half_ in range(2):
                    last = nc.scalar.activation(QH[half_ * KD:(half_ + 1) * KD, h + e, :], query_psum(first)[e * KD:(e + 1) * KD, 0:QW],
                                                ACT.Copy)
            last.then_inc(q_hi, 2)

        def exps(i, h, q, e):
            if e == 0:
                act.wait_ge(row_ready, count(i, h, QT, q + 1))
            part = S[:, h % 2, q, PIECES[e][0]:PIECES[e][1]]
            nc.scalar.activation(part, part, ACT.Exp, bias=negm[:, h % 2, q:q + 1],
                                 accum_out=sums[:, h % 2, q, e:e + 1]).then_inc(probs_ready, 1)

        def take_slot(i, h, s):
            act.wait_ge(transposed, count(i, h, TS, s + 1))
            act.wait_ge(pt_free, count(i, h, TS, ring_used(s)))
            nc.scalar.activation(PT[:, s % RING, :], psT[s % 2][:, :], ACT.Copy).then_inc(pt_act, 1)

        def copy_late(i, h, quadrants):
            act.wait_ge(late_transposed, count(i, h, QT, QT))
            for qi in quadrants:
                src, dst = late_blocks(h, qi, qi)
                nc.scalar.activation(dst, src, ACT.Copy).then_inc(late_copied, 1)

        def step(i, h, nxt, nxt2, prev):
            i1, h1 = (i, h + 1) if h + 1 < GROUP else (i + 1, 0)
            i2, h2 = (i, h + 2) if h + 2 < GROUP else (i + 1, h + 2 - GROUP)
            for c in range(SUBSTEPS):
                take_slot(i, h, 2 * c)
                if c == 0:
                    exps(i, h, 1, NE - 1)
                if c in (1, 2):
                    copy_late(i, h, (2 * c - 2, 2 * c - 1))
                if 2 * c + 1 in ACT_SLOTS:
                    take_slot(i, h, 2 * c + 1)
                if nxt and c >= SUBSTEPS - 2:
                    exps(i1, h1, 0, c - (SUBSTEPS - 2))
                if nxt2 and h % 2 == 0 and c == QUERY_AT:
                    act.wait_ge(scores_ready, count(i, h, SLOTS, SLOTS))
                    query_hi(i2, h2)
            if nxt:
                exps(i1, h1, 0, NE - 1)
                exps(i1, h1, 1, 0)
                exps(i1, h1, 1, 1)
            act.wait_ge(late_used, count(i, h, 1, 1))
            act.wait_ge(o_ready, count(i, h, 1, START))
            nc.scalar.activation(Oodd[:, :], psO[KD:2 * KD, 0:QW], ACT.Copy).then_inc(odd_copied, 1)

        act.sem_inc(v_act, START)
        if norm:
            act.sem_inc(h_ready, START)
            for b in range(2):
                act.sem_inc(h_out[b], 16 * START)
            relu(0, 0)
        chunks(act, keys_values)

        act.sem_inc(pt_act, PT_START)
        for k in range(NE):
            exps(0, 0, 0, k)
        for k in range(NE - 1):
            exps(0, 0, 1, k)
        steps(act, step)

    def vector_program(dve):
        def statistics(i, b):
            dve.wait_ge(x_in[b], i * 16 + 16)
            for r in range(CR):
                nc.vector.bn_stats(stats[:, b, r, :], xb[b][:, r, :]).then_inc(stat1, 1)
            wait_apart(dve, stat1, i * (2 * CR) + (b + 1) * CR, dve_passed)
            for r in range(CR):
                nc.vector.bn_aggr(mv[:, b, r, :], stats[:, b, r, :]).then_inc(aggr, 1)
            dve.wait_ge(aggr, i * (2 * CR) + (b + 1) * CR)
            nc.vector.tensor_scalar(mv[:, b, :, 1], mv[:, b, :, 1], EPS, None, ALU.add).then_inc(var_ready, 1)

        def normalise(i, b):
            dve.wait_ge(rstd_ready, i * 2 + (b + 1))
            for r in range(CR):
                last = nc.vector.tensor_scalar(xb[b][:, r, :], xb[b][:, r, :], mv[:, b, r, 0:1],
                                               rstd[:, b, r:r + 1], ALU.subtract, ALU.mult)
            last.then_inc(normed, 1)

        def keys_values(i, b, nxt, nxt2):
            if norm and nxt:
                normalise(*after(i, b))
            for h in range(GROUP):
                if h == 2 and norm and nxt2:
                    statistics(i + 1, b)
                dve.wait_ge(k_hi, i * (2 * GROUP) + (b * GROUP + h + 1))
                rows = slice(h % 2 * KD, (h % 2 + 1) * KD)
                cols = bass.ds((i * 2 + b) * CH, CH)
                nc.vector.tensor_tensor(K2[KD:2 * KD, h, cols], psK[h // 2][b][rows, :], K2.bitcast(F32)[0:KD, h, cols],
                                        ALU.subtract).then_inc(k_lo, 1)
            if not nxt:
                for e in range(2):
                    query_lo(0, 0, e, True)
            dve.wait_ge(v_proj, i * 4 + (2 * b + 2 + START))
            nc.vector.tensor_copy(V[:, bass.ds((i * 2 + b) * CR + 2, 2), :],
                                  psV[1][:, :].rearrange("p (a n) -> p a n", a=2)).then_inc(v_dve, 1)

        def query_lo(i, h, e, first=False):
            dve.wait_ge(q_hi, count(i, h, 1, 2))
            for half_ in range(2):
                rows = slice(half_ * KD, (half_ + 1) * KD)
                last = nc.vector.tensor_tensor(QL[rows, h + e, :], query_psum(first)[e * KD:(e + 1) * KD, 0:QW],
                                               QH.bitcast(F32)[rows, h + e, :], ALU.subtract)
            last.then_inc(q_lo, 1)

        def mask(i, h, j, first=False):
            q, k = divmod(j, SPT)
            if h == 0 and k == 0:
                dve.wait_ge(bias_ready, i * QT + (q + 1))
            if j == SPT + 1 and not first:
                dve.wait_ge(late_moved, count(i, h, 16 * MOVES, 0))
                dve.wait_ge(late_copied, count(i, h, QUAD, 0))
            wait_apart(dve, scores_ready, count(i, h, SLOTS, j + 1), dve_passed)
            part = S[:, h % 2, q, k * SLOT:(k + 1) * SLOT]
            nc.vector.tensor_tensor_reduce(out=part, in0=psS[j % 2][:, :], in1=B[:, q, k * SLOT:(k + 1) * SLOT],
                                           scale=SCALE, scalar=LOWEST, op0=ALU.add, op1=ALU.max,
                                           accum_out=mx[:, h % 2, q, k:k + 1]).then_inc(slot_masked, 1)
            if k == SPT - 1:
                dve.wait_ge(slot_masked, count(i, h, SLOTS, j + 1))
                own = S[:, h % 2, q, bass.ds(i * QW + q * P, P)]
                nc.vector.tensor_tensor(own, own, diag[:, :], ALU.add)
                nc.vector.tensor_reduce(negm[:, h % 2, q:q + 1], mx[:, h % 2, q, :], AX_X, ALU.max,
                                        negate=True).then_inc(row_ready, 1)

        def take_slot(i, h, s):
            dve.wait_ge(transposed, count(i, h, TS, s + 1))
            dve.wait_ge(pt_free, count(i, h, TS, ring_used(s)))
            nc.vector.tensor_copy(PT[:, s % RING, :], psT[s % 2][:, :]).then_inc(pt_dve, 1)

        def transpose_late(i, h, q, before):
            dve.wait_ge(probs_ready, count(i, h, QT * NE, q * NE + 1))
            if before:
                if q == 0:
                    dve.wait_ge(transposed, count(i, h, TS, 0))
                else:
                    dve.wait_ge(late_used, count(i, h, 1, 0))
            src = S[:, h % 2, q, LC:N].rearrange("p (n b) -> p n b", b=32)
            dst = T1(h)[:, q, :].rearrange("p (j m a) -> p m j a", j=QUAD, a=32)
            nc.vector.transpose(dst, src).then_inc(late_transposed, 1)

        def denominators(i, h):
            dve.wait_ge(probs_ready, count(i, h, QT * NE, QT * NE))
            nc.vector.tensor_reduce(den[:, :], sums[:, h % 2, :, :], AX_X, ALU.add).then_inc(summed, 1)
            dve.wait_ge(summed, count(i, h, 1, 1))
            dve.wait_ge(rden_stored, count(i, h, 16, 16 * START))
            nc.vector.reciprocal(rden[:, :], den[:, :]).then_inc(den_ready, 1)

        def sum_halves(i, h):
            dve.wait_ge(odd_copied, count(i, h, 1, 1))
            nc.vector.tensor_tensor(Oodd[:, :], psO[0:KD, 0:QW], Oodd[:, :], ALU.add).then_inc(o_summed, 1)
            dve.wait_ge(o_summed, count(i, h, 1, 1 + START))
            dve.wait_ge(rden_in, count(i, h, 16, 16))
            dve.wait_ge(projected, count(i, h, 1, START - h % 2))
            half_ = h % 2
            nc.vector.tensor_tensor(O[half_ * KD:(half_ + 1) * KD, :].rearrange("k (q p) -> k q p", q=QT),
                                    Oodd[:, :].rearrange("k (q p) -> k q p", q=QT),
                                    RB[:, :].rearrange("k (p q) -> k q p", q=QT), ALU.mult).then_inc(o_ready, 1)

        def add_heads(i, h):
            dve.wait_ge(projected, count(i, h, 1, 1 + START))
            if h == 1:
                dve.wait_ge(base_in, i * 16 + 16)
            else:
                dve.wait_ge(head_added, count(i, h, 1, START - 1))
            dst = res if h == GROUP - 1 else acc
            nc.vector.tensor_tensor(dst[:, :, :], psP[:, :].rearrange("p (q d) -> p q d", q=QT), acc[:, :, :],
                                    ALU.add).then_inc(head_added, 2)

        def step(i, h, nxt, nxt2, prev):
            i1, h1 = (i, h + 1) if h + 1 < GROUP else (i + 1, 0)
            i2, h2 = (i, h + 2) if h + 2 < GROUP else (i + 1, h + 2 - GROUP)
            for c in range(SUBSTEPS):
                if nxt and c:
                    mask(i1, h1, c + 1)
                if 2 * c + 1 in DVE_SLOTS:
                    take_slot(i, h, 2 * c + 1)
                if prev and h % 2 == 0 and c == PROJECT_AT:
                    add_heads(*last_step(i, h))
                if c == QUERY_AT:
                    denominators(i, h)
                if nxt2 and h % 2 == 0 and c > QUERY_AT:
                    query_lo(i2, h2, c - QUERY_AT - 1)
            if nxt:
                mask(i1, h1, SLOTS - 2)
                mask(i1, h1, SLOTS - 1)
                transpose_late(i1, h1, 0, True)
            if nxt2:
                mask(i2, h2, 0)
            if nxt:
                transpose_late(i1, h1, 1, True)
            if nxt2:
                mask(i2, h2, 1)
            sum_halves(i, h)

        dve.sem_inc(k_lo, 2 * GROUP)
        dve.sem_inc(v_dve, START)
        if norm:
            nc.vector.memset(half[:, :], -0.5).then_inc(half_set, 1)
            statistics(0, 0)
            normalise(0, 0)
            statistics(0, 1)
        chunks(dve, keys_values)

        dve.sem_inc(head_added, START)
        dve.sem_inc(o_summed, START)
        dve.sem_inc(o_ready, START)
        if norm:
            dve.wait_ge(consts, 3)
            for b in range(2):
                dve.wait_ge(h_out[b], 16 * (NC // 2 + START))
        for j in range(SLOTS):
            mask(0, 0, j, first=True)
        for q in range(QT):
            transpose_late(0, 0, q, False)
        mask(0, 1, 0)
        mask(0, 1, 1)
        steps(dve, step)
        add_heads(PAIRS - 1, GROUP - 1)

    return ((sync_program, gpsimd_program, tensor_program, scalar_program, vector_program),
            (late_used, slot_masked, projected, o_summed, head_added))


def build(nc, x, adj, Wk, Wq, Wv, Wo, out):
    hT = nc.dram_tensor("hT_scratch", [P, DC, N], F32, kind="Internal").ap()
    rden_scratch = nc.dram_tensor("rden_scratch", [2, P, QT], F32, kind="Internal").ap()
    partial = nc.dram_tensor("partial_scratch", [N, D], F32, kind="Internal").ap()
    with ExitStack() as ctx:
        def sb(name, shape, dt=F32):
            return ctx.enter_context(nc.sbuf_tensor(name, shape, dt))

        def sem(name):
            return ctx.enter_context(nc.semaphore(name))

        K2 = sb("K2", [P, GROUP, N], F32R)
        V = sb("V", [P, MT, GROUP * KD])
        S = sb("S", [P, 2, QT, N])
        B = sb("B", [P, QT, N], BF16)
        PT = sb("PT", [P, RING, 2 * QW])
        QH = sb("QH", [P, GROUP, QW], F32R)
        QL = sb("QL", [P, GROUP, QW], F32R)
        hq = sb("hq", [P, DC, QW])
        wq = sb("wq", [P, DC, GROUP * KD])
        wo = sb("wo", [P, GROUP // 2, D])
        O = sb("O", [P, QW])
        Oodd = sb("Oodd", [KD, QW])
        RB = sb("RB", [KD, QW])
        acc = sb("acc", [P, QT, D])
        res = sb("res", [P, QT, D])
        ident = sb("ident", [P, P])
        notI = sb("notI", [P, P], BF16)
        diag = sb("diag", [P, P])
        mx = sb("mx", [P, 2, QT, SPT])
        negm = sb("negm", [P, 2, QT])
        sums = sb("sums", [P, 2, QT, NE])
        den = sb("den", [P, QT])
        rden = sb("rden", [P, QT])
        stats = sb("stats", [P, 2, CR, 6])
        mv = sb("mv", [P, 2, CR, 2])
        rstd = sb("rstd", [P, 2, CR])
        half = sb("half", [P, CR])
        psS = [ctx.enter_context(nc.psum_tensor(f"psS{j}", [P, SLOT], F32)) for j in range(2)]
        psT = [ctx.enter_context(nc.psum_tensor(f"psT{j}", [P, BANK], F32)) for j in range(2)]
        psO = ctx.enter_context(nc.psum_tensor("psO", [P, BANK], F32))
        psP = ctx.enter_context(nc.psum_tensor("psP", [P, BANK], F32))

        xb = [S[:, 1, 0, b * 1024:(b + 1) * 1024].rearrange("p (r d) -> p r d", d=D) for b in range(2)]
        hc = [S[:, 0, 0, b * 1024:(b + 1) * 1024].rearrange("p (c n) -> p c n", c=DC) for b in range(2)]
        wk = S[:, 0, 1, 0:512].rearrange("p (c n) -> p c n", c=DC)
        wv = S[:, 0, 1, 512:1024].rearrange("p (c n) -> p c n", c=DC)

        ones_set, consts = sem("ones_set"), sem("consts")
        tiles = (K2, V, S, B, PT, QH, QL, hq, wq, wo, O, Oodd, RB, acc, res, ident, notI, diag, mx, negm, sums, den, rden,
                 stats, mv, rstd, half, xb, hc, wk, wv, psS, psT, psO, psP, rden_scratch, ones_set, consts)
        programs, before = [], None
        for g in range(GROUPS):
            program, before = group_programs(nc, sem, g, before, x, hT, adj, Wk, Wq, Wv, Wo, x if g == 0 else partial,
                                             out if g == GROUPS - 1 else partial, tiles)
            programs.append(program)
        with nc.Block() as block:
            @block.sync
            def _(sp):
                for sync_program, _, _, _, _ in programs:
                    sync_program(sp)

            @block.gpsimd
            def _(pool):
                for _, gpsimd_program, _, _, _ in programs:
                    gpsimd_program(pool)

            @block.tensor
            def _(pe):
                for _, _, tensor_program, _, _ in programs:
                    tensor_program(pe)

            @block.scalar
            def _(act):
                for _, _, _, scalar_program, _ in programs:
                    scalar_program(act)

            @block.vector
            def _(dve):
                for _, _, _, _, vector_program in programs:
                    vector_program(dve)


def kernel(x, adj, L0_gnn_Wks, L0_gnn_Wqs, L0_gnn_Wvs, L0_gnn_Wo):
    import concourse.bacc as bacc
    import numpy as np
    from concourse.bass_utils import run_bass_kernel_spmd

    nc = bacc.Bacc("TRN2", target_bir_lowering=False, num_devices=1)
    arrays, args = {}, []
    for name, a in (("x", x), ("adj", adj), ("Wk", L0_gnn_Wks), ("Wq", L0_gnn_Wqs), ("Wv", L0_gnn_Wvs), ("Wo", L0_gnn_Wo)):
        a = np.ascontiguousarray(a)
        arrays[f"in_{name}"] = a
        args.append(nc.dram_tensor(f"in_{name}", a.shape, mybir.dt.from_np(a.dtype), kind="ExternalInput").ap())
    out = nc.dram_tensor("out", [N, D], F32, kind="ExternalOutput").ap()
    build(nc, *args, out)
    r = run_bass_kernel_spmd(nc, [arrays], core_ids=[0])
    return r.results[0]["out"]
```
